# Optimizing a Trainium2 kernel written in Bass

```python
import numpy as np
import jax
import jax.numpy as jnp

def _softmax(x, axis=-1):
    return jax.nn.softmax(x, axis=axis)

def _gelu(x):
    return jax.nn.gelu(x, approximate=True)

def _silu(x):
    return jax.nn.silu(x)

def _sigmoid(x):
    return jax.nn.sigmoid(x)

def _layernorm(x, axis=-1, eps=1e-05):
    m = jnp.mean(x, axis=axis, keepdims=True)
    v = jnp.var(x, axis=axis, keepdims=True)
    return (x - m) / jnp.sqrt(v + eps)

def _scatter_add(tgt, idx, src, axis=0):
    return tgt.at[idx].add(src)

def _segment_sum(src, seg, n):
    return jax.ops.segment_sum(src, seg, n)
kernel_name = 'mk_lm_tower_d1_tok_ids256_r4_b8b5ad'

def setup_inputs(seed: int=0):
    np.random.seed(seed)
    _w = jnp.asarray

    def _rec_inputs():
        import jax
        import jax.numpy as jnp
        _rk = jax.random.key(seed)
        x = jax.random.randint(jax.random.fold_in(_rk, 1), (8, 2048), 0, 64, jnp.int32)
        return x
    x = _rec_inputs()

    def _L0_tok_setup():
        import jax, jax.numpy as jnp
        import numpy as np
        B, T, D = (32, 1024, 64)
        LN_EPS = 1e-05
        key = jax.random.key(seed)
        k0, k1, k2 = jax.random.split(key, 3)
        byte_ids = jax.random.randint(k0, (B, T), 0, 64, dtype=jnp.int32)
        freq_bands = jnp.ones((D // 2,), jnp.float32)
        w1 = jax.random.normal(k1, (D, 2 * D), jnp.float32) * (1.0 / np.sqrt(D))
        b1 = jnp.zeros((2 * D,), jnp.float32)
        gamma = jnp.ones((2 * D,), jnp.float32)
        beta = jnp.zeros((2 * D,), jnp.float32)
        w2 = jax.random.normal(k2, (2 * D, D), jnp.float32) * (1.0 / np.sqrt(2 * D))
        b2 = jnp.zeros((D,), jnp.float32)
        return dict(byte_ids=byte_ids, freq_bands=freq_bands, w1=w1, b1=b1, gamma=gamma, beta=beta, w2=w2, b2=b2)
    _L0_tok_all = _L0_tok_setup()
    _L0_tok_in = {k: v for k, v in _L0_tok_all.items() if k in ('freq_bands', 'w1', 'b1', 'gamma', 'beta', 'w2', 'b2')}
    del _L0_tok_all

    def _L0_attn_setup():
        import jax, jax.numpy as jnp
        import numpy as np
        S, B, D, H, DH = (128, 32, 64, 8, 32)
        LN_EPS = 1e-05

        def elu_p1(x):
            return jax.nn.elu(x) + 1.0

        def sum_norm(x):
            return x / jnp.sum(x, axis=-1, keepdims=True)

        def layer_norm(x, g, b):
            mu = jnp.mean(x, axis=-1, keepdims=True)
            var = jnp.mean(jnp.square(x - mu), axis=-1, keepdims=True)
            return (x - mu) * jax.lax.rsqrt(var + LN_EPS) * g + b

        def _fast_rnn_forward(x, slow_W, out_W, ln_g, ln_b):
            slen, bsz, _ = x.shape
            o = layer_norm(x, ln_g, ln_b)
            qkv = jnp.einsum('sbd,ed->sbe', o, slow_W)
            qkv = qkv.reshape(slen, bsz, H, 5 * DH + 2)
            q, k, v, rk, rv, beta, rbeta = jnp.split(qkv, [DH, 2 * DH, 3 * DH, 4 * DH, 5 * DH, 5 * DH + 1], axis=-1)
            beta = jax.nn.sigmoid(beta)
            rbeta = jax.nn.sigmoid(rbeta)
            q = sum_norm(elu_p1(q))
            k = sum_norm(elu_p1(k))
            rk = jax.nn.softmax(rk, axis=-1)

            def ff_step(W, inp):
                qt, kt, vt, bt = inp
                v_old = jnp.einsum('bhij,bhj->bhi', W, kt)
                W = W + (bt * (vt - v_old))[..., :, None] * kt[..., None, :]
                z = jnp.einsum('bhij,bhj->bhi', W, qt)
                return (W, z)
            W0 = jnp.zeros((bsz, H, DH, DH), x.dtype)
            _, z = jax.lax.scan(ff_step, W0, (q, k, v, beta))

            def rec_step(carry, inp):
                R, h = carry
                zt, kt, vt, bt = inp
                q_rec = jax.nn.softmax(h, axis=-1)
                v_old = jnp.einsum('bhij,bhj->bhi', R, kt)
                R = R + (bt * (vt - v_old))[..., :, None] * kt[..., None, :]
                h = zt + jnp.einsum('bhij,bhj->bhi', R, q_rec)
                return ((R, h), h)
            R0 = jnp.zeros((bsz, H, DH, DH), x.dtype)
            h0 = jnp.zeros((bsz, H, DH), x.dtype)
            _, hs = jax.lax.scan(rec_step, (R0, h0), (z, rk, rv, rbeta))
            out = hs.reshape(slen, bsz, H * DH)
            out = jnp.einsum('sbe,de->sbd', out, out_W)
            return x + out
        key = jax.random.key(seed)
        k1, k2, k3 = jax.random.split(key, 3)
        x = jax.random.normal(k1, (S, B, D), jnp.float32)
        slow_W = jax.random.normal(k2, (H * (5 * DH + 2), D), jnp.float32) * 0.02
        out_W = jax.random.normal(k3, (D, H * DH), jnp.float32) * 0.02
        ln_g = jnp.ones((D,), jnp.float32)
        ln_b = jnp.zeros((D,), jnp.float32)
        return {'x': x, 'slow_W': slow_W, 'out_W': out_W, 'ln_g': ln_g, 'ln_b': ln_b}
    _L0_attn_all = _L0_attn_setup()
    _L0_attn_in = {k: v for k, v in _L0_attn_all.items() if k in ('slow_W', 'out_W', 'ln_g', 'ln_b')}
    del _L0_attn_all

    def _L0_ffn_setup():
        import jax, jax.numpy as jnp
        import numpy as np
        B, S, H, F, E, K = (8, 1024, 64, 128, 16, 2)
        EPS = 1e-05
        key = jax.random.key(seed)
        ks = jax.random.split(key, 9)
        sc = 0.02
        return {'x': jax.random.normal(ks[0], (B, S, H), dtype=jnp.float32), 'gate_w': jax.random.normal(ks[1], (H, E), dtype=jnp.float32) * sc, 'gate_b': jnp.zeros((E,), dtype=jnp.float32), 'w1': jax.random.normal(ks[2], (E, H, F), dtype=jnp.float32) * sc, 'b1': jnp.zeros((E, F), dtype=jnp.float32), 'w2': jax.random.normal(ks[3], (E, F, H), dtype=jnp.float32) * sc, 'b2': jnp.zeros((E, H), dtype=jnp.float32), 'gamma': jnp.ones((H,), dtype=jnp.float32), 'beta': jnp.zeros((H,), dtype=jnp.float32)}
    _L0_ffn_all = _L0_ffn_setup()
    _L0_ffn_in = {k: v for k, v in _L0_ffn_all.items() if k in ('gate_w', 'gate_b', 'w1', 'b1', 'w2', 'b2', 'gamma', 'beta')}
    del _L0_ffn_all
    return {'x': x, 'L0_tok_freq_bands': _L0_tok_in['freq_bands'], 'L0_tok_w1': _L0_tok_in['w1'], 'L0_tok_b1': _L0_tok_in['b1'], 'L0_tok_gamma': _L0_tok_in['gamma'], 'L0_tok_beta': _L0_tok_in['beta'], 'L0_tok_w2': _L0_tok_in['w2'], 'L0_tok_b2': _L0_tok_in['b2'], 'L0_attn_slow_W': _L0_attn_in['slow_W'], 'L0_attn_out_W': _L0_attn_in['out_W'], 'L0_attn_ln_g': _L0_attn_in['ln_g'], 'L0_attn_ln_b': _L0_attn_in['ln_b'], 'L0_ffn_gate_w': _L0_ffn_in['gate_w'], 'L0_ffn_gate_b': _L0_ffn_in['gate_b'], 'L0_ffn_w1': _L0_ffn_in['w1'], 'L0_ffn_b1': _L0_ffn_in['b1'], 'L0_ffn_w2': _L0_ffn_in['w2'], 'L0_ffn_b2': _L0_ffn_in['b2'], 'L0_ffn_gamma': _L0_ffn_in['gamma'], 'L0_ffn_beta': _L0_ffn_in['beta']}

def reference(x, L0_tok_freq_bands, L0_tok_w1, L0_tok_b1, L0_tok_gamma, L0_tok_beta, L0_tok_w2, L0_tok_b2, L0_attn_slow_W, L0_attn_out_W, L0_attn_ln_g, L0_attn_ln_b, L0_ffn_gate_w, L0_ffn_gate_b, L0_ffn_w1, L0_ffn_b1, L0_ffn_w2, L0_ffn_b2, L0_ffn_gamma, L0_ffn_beta):
    import jax
    import jax.numpy as jnp

    def _L0_tok_ref(byte_ids, freq_bands, w1, b1, gamma, beta, w2, b2):
        import jax, jax.numpy as jnp
        import numpy as np
        B, T, D = (32, 1024, 64)
        LN_EPS = 1e-05
        Bsz, Tlen = byte_ids.shape
        Dm = w1.shape[0]
        k = min(Dm // 2, Tlen // 2)
        signal = byte_ids.astype(jnp.float32) / 127.5 - 1.0
        X = jnp.fft.fft(signal, axis=1)[:, :k]
        mag = jnp.abs(X) * freq_bands[:k]
        phase0 = jnp.angle(X)
        pos = jnp.arange(Tlen, dtype=jnp.float32)
        f = jnp.arange(k, dtype=jnp.float32)
        shift = 2.0 * np.pi / Tlen * pos[:, None] * f[None, :]
        phase = phase0[:, None, :] + shift[None, :, :]
        mag_bt = jnp.broadcast_to(mag[:, None, :], (Bsz, Tlen, k))
        feats = jnp.concatenate([mag_bt, jnp.sin(phase), jnp.cos(phase)], axis=-1)
        if feats.shape[-1] < Dm:
            feats = jnp.pad(feats, ((0, 0), (0, 0), (0, Dm - feats.shape[-1])))
        else:
            feats = feats[..., :Dm]
        h = feats @ w1 + b1
        mu = jnp.mean(h, axis=-1, keepdims=True)
        var = jnp.var(h, axis=-1, keepdims=True)
        h = (h - mu) * jax.lax.rsqrt(var + LN_EPS) * gamma + beta
        h = jax.nn.gelu(h, approximate=False)
        return h @ w2 + b2

    def _L0_attn_ref(x, slow_W, out_W, ln_g, ln_b):
        import jax, jax.numpy as jnp
        import numpy as np
        S, B, D, H, DH = (128, 32, 64, 8, 32)
        LN_EPS = 1e-05

        def elu_p1(x):
            return jax.nn.elu(x) + 1.0

        def sum_norm(x):
            return x / jnp.sum(x, axis=-1, keepdims=True)

        def layer_norm(x, g, b):
            mu = jnp.mean(x, axis=-1, keepdims=True)
            var = jnp.mean(jnp.square(x - mu), axis=-1, keepdims=True)
            return (x - mu) * jax.lax.rsqrt(var + LN_EPS) * g + b

        def _fast_rnn_forward(x, slow_W, out_W, ln_g, ln_b):
            slen, bsz, _ = x.shape
            o = layer_norm(x, ln_g, ln_b)
            qkv = jnp.einsum('sbd,ed->sbe', o, slow_W)
            qkv = qkv.reshape(slen, bsz, H, 5 * DH + 2)
            q, k, v, rk, rv, beta, rbeta = jnp.split(qkv, [DH, 2 * DH, 3 * DH, 4 * DH, 5 * DH, 5 * DH + 1], axis=-1)
            beta = jax.nn.sigmoid(beta)
            rbeta = jax.nn.sigmoid(rbeta)
            q = sum_norm(elu_p1(q))
            k = sum_norm(elu_p1(k))
            rk = jax.nn.softmax(rk, axis=-1)

            def ff_step(W, inp):
                qt, kt, vt, bt = inp
                v_old = jnp.einsum('bhij,bhj->bhi', W, kt)
                W = W + (bt * (vt - v_old))[..., :, None] * kt[..., None, :]
                z = jnp.einsum('bhij,bhj->bhi', W, qt)
                return (W, z)
            W0 = jnp.zeros((bsz, H, DH, DH), x.dtype)
            _, z = jax.lax.scan(ff_step, W0, (q, k, v, beta))

            def rec_step(carry, inp):
                R, h = carry
                zt, kt, vt, bt = inp
                q_rec = jax.nn.softmax(h, axis=-1)
                v_old = jnp.einsum('bhij,bhj->bhi', R, kt)
                R = R + (bt * (vt - v_old))[..., :, None] * kt[..., None, :]
                h = zt + jnp.einsum('bhij,bhj->bhi', R, q_rec)
                return ((R, h), h)
            R0 = jnp.zeros((bsz, H, DH, DH), x.dtype)
            h0 = jnp.zeros((bsz, H, DH), x.dtype)
            _, hs = jax.lax.scan(rec_step, (R0, h0), (z, rk, rv, rbeta))
            out = hs.reshape(slen, bsz, H * DH)
            out = jnp.einsum('sbe,de->sbd', out, out_W)
            return x + out
        return _fast_rnn_forward(x, slow_W, out_W, ln_g, ln_b)

    def _L0_ffn_ref(x, gate_w, gate_b, w1, b1, w2, b2, gamma, beta):
        import jax, jax.numpy as jnp
        import numpy as np
        B, S, H, F, E, K = (8, 1024, 64, 128, 16, 2)
        EPS = 1e-05
        gate_logits = x @ gate_w + gate_b
        topk_vals, topk_idx = jax.lax.top_k(gate_logits, K)
        topk_w = jax.nn.softmax(topk_vals, axis=-1)
        h = jax.nn.relu(jnp.einsum('bsh,ehf->bsef', x, w1) + b1)
        expert_out = jnp.einsum('bsef,efh->bseh', h, w2) + b2
        sel = jnp.take_along_axis(expert_out, topk_idx[:, :, :, None], axis=2)
        moe = jnp.sum(topk_w[..., None] * sel, axis=2)
        y = x + moe
        mu = jnp.mean(y, axis=-1, keepdims=True)
        var = jnp.var(y, axis=-1, keepdims=True)
        return (y - mu) / jnp.sqrt(var + EPS) * gamma + beta
    h = _L0_tok_ref(x, L0_tok_freq_bands, L0_tok_w1, L0_tok_b1, L0_tok_gamma, L0_tok_beta, L0_tok_w2, L0_tok_b2)
    h = h + _L0_attn_ref(_layernorm(h, axis=-1), L0_attn_slow_W, L0_attn_out_W, L0_attn_ln_g, L0_attn_ln_b)
    h = h + _L0_ffn_ref(_layernorm(h, axis=-1), L0_ffn_gate_w, L0_ffn_gate_b, L0_ffn_w1, L0_ffn_b1, L0_ffn_w2, L0_ffn_b2, L0_ffn_gamma, L0_ffn_beta)
    return h

_drawn_inputs = setup_inputs


def setup_inputs(seed=0):
    import zlib

    import numpy as np

    out = dict(_drawn_inputs(seed))
    spreads = {'L0_tok_freq_bands': (1.0, 0.6),
     'L0_tok_b1': (0.0, 0.8),
     'L0_tok_gamma': (1.0, 0.2),
     'L0_tok_beta': (0.0, 0.1),
     'L0_tok_b2': (0.0, 0.1),
     'L0_attn_ln_g': (1.0, 0.6),
     'L0_attn_ln_b': (0.0, 0.8),
     'L0_ffn_gate_b': (0.0, 0.1),
     'L0_ffn_b1': (0.0, 0.8),
     'L0_ffn_b2': (0.0, 0.364),
     'L0_ffn_gamma': (1.0, 0.2),
     'L0_ffn_beta': (0.0, 0.1)}
    factors = {'L0_attn_slow_W': 8.0,
     'L0_attn_out_W': 8.0,
     'L0_ffn_gate_w': 2.947,
     'L0_ffn_w1': 8.0,
     'L0_ffn_w2': 8.0}
    for name, (base, spread) in spreads.items():
        noise = np.random.default_rng([zlib.crc32(name.encode()), seed]).standard_normal(out[name].shape)
        drawn = base * np.exp(spread * noise) if base else spread * noise
        out[name] = jnp.asarray(drawn.astype(out[name].dtype))
    for name, factor in factors.items():
        out[name] = (out[name] * factor).astype(out[name].dtype)
    return out
```

```python
from contextlib import ExitStack

import concourse.bass as bass
from concourse import mybir

P = 128
ROWS, T = 8, 2048
NT = T // P
D = 64
BINS = 32
HID = 128
H, DH = 8, 32
HD = H * DH
E, F = 16, 128
FEATS = 3 * BINS + 1
SLOW = H * (5 * DH + 2)
SLOW_CHUNK, SLOW_CHUNKS = 108, 12
EPS = 1e-5
RSQRT_SEED = float(0x5F3759DF)
NEWTON = 3
RSQRT = 2 + 3 * NEWTON
NORM = 7 + RSQRT
BIG = 3.0e38
TC = T // P
GROUPS = 2
GROWS = ROWS // GROUPS
FFN_STEPS = E * GROUPS
FFN_SLOTS = FFN_STEPS + 2
FFN_EARLY = 10
FFN_MID = 20
GX_RING = 3

F32 = mybir.dt.float32
I32 = mybir.dt.int32
ALU = mybir.AluOpType
ACT = mybir.ActivationFunctionType
AX = mybir.AxisListType.X

EV_HST, EV_RK, EV_XFT, EV_GT, EV_OT, EV_KQ, EV_V, EV_RV = 0, 4, 8, 10, 11, 12, 20, 28
EVENTS = 32
PROLOGUE = EVENTS - EV_OT
SKIPPED = 4 + 2 + 1


def is_first(t):
    return isinstance(t, int) and t == 0


def fill(t, ev):
    if isinstance(t, int) and t < 0:
        return ev - EV_OT
    if is_first(t):
        return PROLOGUE + (ev - EV_RK if ev < EV_XFT else ev - SKIPPED)
    if isinstance(t, int) and t == NT:
        return PROLOGUE - SKIPPED + EVENTS * NT - PROLOGUE + (ev if ev < EV_XFT else ev - 4)
    return t * EVENTS + (PROLOGUE - SKIPPED + ev)


def parity(t, ev):
    return fill(t, ev) % 2 if isinstance(t, int) else (PROLOGUE - SKIPPED + ev) % 2

STEPS = dict(encode=4 + RSQRT, front=NORM + 6 + RSQRT, mix=7, dots=18, rkprep=2, rknorm=3, rdots=16, back=NORM + 2, gates=19,
             init=2, delta=16, rdelta=14, rec=68, tail=NORM + 5)


class Stage:

    def __init__(self, eng, sem, name, tile):
        self.eng, self.sem, self.name, self.n = eng, sem, name, 0
        self.base = tile * STEPS[name]

    def did(self, ins):
        ins.then_inc(self.sem, 1)
        self.n += 1

    def settle(self):
        self.eng.wait_ge(self.sem, self.base + self.n)

    def then(self, ins):
        self.did(ins)
        self.settle()

    def close(self):
        self.settle()
        assert self.n == STEPS[self.name], (self.name, self.n)


GATE_EXP = 13
SORTS = 8


def REC_EXP(i):
    return 7 + 9 * i


def wait(eng, sem, value):
    if not (isinstance(value, int) and value <= 0):
        eng.wait_ge(sem, value)


def build(nc, x, freq, tw1, tb1, tgam, tbet, tw2, tb2, slow, outw, lng, lnb, gw, gb, fw1, fb1, fw2, fb2,
          fgam, fbet, dft_d, phase_d, ident_d, rank_d, out):
    ctx = ExitStack()
    with ctx:
        def sb(name, shape, dt=F32):
            return ctx.enter_context(nc.sbuf_tensor(name, shape, dt))

        def sem(name):
            return ctx.enter_context(nc.semaphore(name))

        bank = [ctx.enter_context(nc.psum_tensor(f"bank{i}", [P, 512], F32)) for i in range(8)]
        gx_ps = bank[0]
        l1_ps = bank[1:3]
        y_ps = bank[3:5]
        prj_ps = bank[5:7]
        vec_ps = bank[7]

        h_all = sb("h_all", [P, NT, ROWS, D])
        ident = sb("ident", [P, P])
        rank = sb("rank", [P, E])
        slowT = sb("slowT", [P, SLOW])
        KQC, VC, RVC, RKC = 0, 2 * HD, 3 * HD + 2 * H, 4 * HD + 2 * H
        outT = sb("outT", [P, 2, D])
        lngb = sb("lngb", [P, 2])
        gate_w = sb("gate_w", [D, E])
        gate_b = sb("gate_b", [P, E])
        w1 = sb("w1", [D + 1, E, F])
        w2 = sb("w2", [F, E, D])
        b2rows = sb("b2rows", [P, ROWS, D])
        gamb = sb("gamb", [P, 2, D])

        kq = sb("kq", [P, H, 2 * ROWS, DH])
        ex = sb("ex", [P, H, 2 * ROWS, DH])
        prod = sb("prod", [P, H, 2 * ROWS, DH])
        acc = sb("acc", [P, H, 2 * ROWS, DH])
        v = sb("v", [P, H, ROWS, DH])
        rv = sb("rv", [P, H, ROWS, DH])
        rk = sb("rk", [P, H, ROWS + 1, DH])
        ru = sb("ru", [P, H, ROWS, DH])
        hs = sb("hs", [P, ROWS, H, DH])
        hsT = ru[:].rearrange("p h s d -> p (h s d)").rearrange("p (c n) -> p c n", c=2 * ROWS)
        dots = sb("dots", [P, H, ROWS, 2 * ROWS])
        rdots = sb("rdots", [P, H, ROWS, ROWS])
        be = sb("be", [P, ROWS, 2, H])
        br = sb("br", [P, ROWS, 2, H])
        ksum = sb("ksum", [P, H, 2 * ROWS])
        ik = sb("ik", [P, H, 2 * ROWS])
        mk = sb("mk", [P, H, 2 * ROWS])
        rkm = sb("rkm", [P, H, ROWS])
        rks = sb("rks", [P, H, ROWS])
        nrb = sb("nrb", [P, H, ROWS])
        eh = sb("eh", [P, H, DH])
        ht = sb("ht", [P, H, DH])
        qd = sb("qd", [P, H, ROWS + 1])
        qr = sb("qr", [P, H])
        hmax = sb("hmax", [P, H])

        cen = sb("cen", [P, ROWS, D])
        sqr = sb("sqr", [P, ROWS, D])
        onorm = sb("onorm", [P, ROWS, D])
        oT = sb("oT", [P, ROWS // 2, P])
        st = sb("st", [P, 8, ROWS])
        hb = sb("hb", [P, ROWS, D])
        xf = sb("xf", [P, ROWS, D + 1])
        xfT = sb("xfT", [D, ROWS, P])
        lg = sb("lg", [P, 6, ROWS, E])
        gt = sb("gt", [P, 8, ROWS])
        g = sb("g", [P, ROWS, E])
        gT = sb("gT", [P, P])
        gx = [sb(f"gx{i}", [P, ROWS, D + 1]) for i in range(GX_RING)]
        gxT = [sb(f"gxT{i}", [D + 1, 512]) for i in range(2)]
        hT = [sb(f"hT{i}", [F, 512]) for i in range(2)]
        ysb = xfT
        yo = sb("yo", [P, ROWS, D])

        phase = ex[0:FEATS].rearrange("p h s d -> p (h s d)")[:, 0:T + P]
        phase_now = hs[0:FEATS].rearrange("p s h d -> p (s h d)")[:, 0:P]
        flat_v = v[:].rearrange("p h s d -> p (h s d)")
        flat_rv = rv[:].rearrange("p h s d -> p (h s d)")
        flat_ru = ru[:].rearrange("p h s d -> p (h s d)")
        flat_kq = kq[:].rearrange("p h s d -> p (h s d)")
        flat_prod = prod[:].rearrange("p h s d -> p (h s d)")
        flat_acc = acc[:].rearrange("p h s d -> p (h s d)")
        dft = flat_prod[:, 0:TC * 2 * 3 * BINS].rearrange("p (c n) -> p c n", c=TC)
        wb = flat_kq[0:FEATS, 0:ROWS * HID]
        sq_enc = flat_kq[:, 1024:2048]
        hn_enc = flat_kq[:, 2048:3072]
        ge_enc = flat_kq[:, 3072:4096]
        w1ext = flat_rv[0:FEATS, 0:HID]
        w2e = flat_rv[:, 128:192]
        b2e = flat_rv[:, 192:256]
        cs = flat_rv[0:FEATS, 256:264]
        fb = flat_rv[2 * BINS:3 * BINS, 264:265]
        gam_enc = flat_rv[:, 265:266]
        bet_enc = flat_rv[:, 266:267]
        wmean = flat_rv[0:FEATS, 267:268]
        re_im = flat_rv[0:3 * BINS, 272:288]
        tmp8 = [flat_rv[0:3 * BINS, 288 + 8 * i:296 + 8 * i] for i in range(5)]
        rs_enc = [flat_rv[:, 336 + 8 * i:344 + 8 * i] for i in range(3)]
        sig = flat_rv[:, 384:512].rearrange("p (b c) -> p b c", b=ROWS)
        ids = ctx.enter_context(nc.sbuf_tensor("ids", [P, ROWS, TC], I32))
        slow_raw = flat_acc[0:SLOW_CHUNK, 0:SLOW_CHUNKS * 2 * D].rearrange("p (c a d) -> p c a d", c=SLOW_CHUNKS, a=2)
        slowT_raw = flat_ru[:, 0:SLOW]
        outw_raw = flat_v[0:D, 0:HD]

        loaded = sem("loaded")
        b2_cleared = sem("b2_cleared")
        b2_loaded = sem("b2_loaded")
        setup_steps = sem("setup_steps")
        bins_summed = sem("bins_summed")
        bins_copied = sem("bins_copied")
        slow_turned = sem("slow_turned")
        slow_copied = sem("slow_copied")
        slow_sorted = sem("slow_sorted")
        outw_turned = sem("outw_turned")
        phase_copied = sem("phase_copied")
        hid_summed = sem("hid_summed")
        hid_squared = sem("hid_squared")
        hid_turned = sem("hid_turned")
        hid_gelu = sem("hid_gelu")
        token_summed = sem("token_summed")
        token_stored = sem("token_stored")
        v_did = {name: sem("v_" + name) for name in STEPS}
        prj_full = sem("prj_full")
        prj_taken = sem("prj_taken")
        vec_full = sem("vec_full")
        rk_exp = sem("rk_exp")
        h_exp = sem("h_exp")
        gate_exp = sem("gate_exp")
        gx_ready = sem("gx_ready")
        gx_turned = sem("gx_turned")
        gxT_ready = sem("gxT_ready")
        l1_done = sem("l1_done")
        hT_ready = sem("hT_ready")
        l2_done = sem("l2_done")
        y_copied = sem("y_copied")
        z_cleared = sem("z_cleared")
        out_stored = sem("out_stored")

        block = ctx.enter_context(nc.Block())
        N_LOADS = 28
        SETUP_V = 20 + RSQRT + ROWS

        def row(a):
            return a.rearrange("(a n) -> a n", a=1)

        def col(a):
            return a.rearrange("(n a) -> n a", a=1)

        def of_tile(t):
            return h_all[:, bass.ds(t, 1)].rearrange("p a b d -> p (a b) d")

        def done(eng, stage, tiles):
            wait(eng, v_did[stage], tiles * STEPS[stage])

        @block.sync
        def _(sp):
            n = [0]

            def load(dst, src):
                sp.dma_start(dst, src).then_inc(loaded, 16)
                n[0] += 1

            load(ids[:], x.rearrange("b (p c) -> p b c", c=TC))
            load(dft, dft_d)
            load(w1ext[0:BINS], tw1[BINS:2 * BINS, :])
            load(w1ext[BINS:2 * BINS], tw1[BINS:2 * BINS, :])
            load(w1ext[2 * BINS:3 * BINS], tw1[0:BINS, :])
            load(w1ext[3 * BINS:FEATS], row(tb1))
            load(fb, col(freq))
            load(phase, phase_d)
            load(ident[:], ident_d)
            load(gam_enc, col(tgam))
            load(bet_enc, col(tbet))
            load(w2e, tw2)
            load(b2e, row(tb2).broadcast_to([P, D]))
            load(slow_raw[:, :, 0, :], slow.rearrange("(c p) d -> p c d", p=SLOW_CHUNK))
            load(slow_raw[:, :, 1, :], slow.rearrange("(c p) d -> p c d", p=SLOW_CHUNK))
            load(outw_raw, outw)
            for half in (0, D):
                load(lngb[half:half + D, 0:1], col(lng))
                load(lngb[half:half + D, 1:2], col(lnb))
            load(rank[:], row(rank_d).broadcast_to([P, E]))
            load(gate_w[:], gw)
            load(gate_b[:], row(gb).broadcast_to([P, E]))
            load(w1[0:D], fw1.rearrange("e h f -> h e f"))
            load(w1[D:D + 1], fb1.unsqueeze(0))
            load(w2[:], fw2.rearrange("e f h -> f e h"))
            load(gamb[:, 0, :], row(fgam).broadcast_to([P, D]))
            load(gamb[:, 1, :], row(fbet).broadcast_to([P, D]))
            assert n[0] == N_LOADS, n
            sp.wait_ge(b2_cleared, 1)
            for r in range(ROWS):
                sp.dma_start(b2rows[r * E:(r + 1) * E, r, :], fb2).then_inc(b2_loaded, 16)

            with sp.Fori(0, NT) as t:
                sp.wait_ge(v_did["tail"], t * STEPS["tail"] + STEPS["tail"])
                sp.dma_start(out[:, bass.ds(t * P, P), :].rearrange("b p d -> p b d"), yo[:]).then_inc(out_stored, 16)
            sp.wait_ge(out_stored, 16 * NT)

        @block.gpsimd
        def _(pool):
            pool.memset(b2rows[:], 0.0).then_inc(b2_cleared, 1)

            def clear_z(t):
                done(pool, "rec", t)
                one = ident[:, 0:1].unsqueeze(2).unsqueeze(3).broadcast_to([P, H, ROWS, DH])
                pool.tensor_tensor(acc[:, :, 1:2 * ROWS:2, :], one, one, ALU.subtract).then_inc(z_cleared, 1)

            def gate_inputs(t):
                done(pool, "gates", t + 1)
                for e in range(E):
                    wait(pool, gx_turned, t * FFN_STEPS + GROUPS * (e - GX_RING + 1))
                    pool.tensor_tensor(gx[e % GX_RING][:], xf[:],
                                       g[:, :, e:e + 1].broadcast_to([P, ROWS, D + 1]), ALU.mult).then_inc(gx_ready, 1)

            pool.wait_ge(loaded, 16 * N_LOADS)
            pool.wait_ge(slow_turned, SLOW_CHUNKS)
            clear_z(0)
            clear_z(1)
            gate_inputs(0)
            with pool.Fori(1, NT - 1) as t:
                clear_z(t + 1)
                gate_inputs(t)
            gate_inputs(NT - 1)

        @block.vector
        def _(dve):
            V = nc.vector

            def stage(name, t):
                return Stage(dve, v_did[name], name, t)

            def over_d(y, n=D):
                return y.unsqueeze(2).broadcast_to([P, ROWS, n])

            def norm(a, src):
                a.then(V.tensor_reduce(st[:, 0], src, AX, ALU.add))
                a.then(V.tensor_scalar(st[:, 1], st[:, 0], 1.0 / D, None, ALU.mult))
                a.then(V.tensor_tensor(cen[:], src, over_d(st[:, 1]), ALU.subtract))
                a.then(V.tensor_tensor(sqr[:], cen[:], cen[:], ALU.mult))
                a.then(V.tensor_reduce(st[:, 0], sqr[:], AX, ALU.add))
                a.then(V.tensor_scalar(st[:, 2], st[:, 0], 1.0 / D, None, ALU.mult))
                a.then(V.tensor_scalar(st[:, 1], st[:, 2], EPS, None, ALU.add))
                rsqrt(a.then, st[:, 3], st[:, 1], st[:, 0])

            def rsqrt(then, y, x, t):
                then(V.tensor_scalar(t.bitcast(I32), x.bitcast(I32), 1, None, ALU.logical_shift_right))
                then(V.tensor_scalar(y.bitcast(I32), t.bitcast(I32), -1.0, RSQRT_SEED, ALU.mult, ALU.add))
                for _ in range(NEWTON):
                    then(V.tensor_tensor(t, y, y, ALU.mult))
                    then(V.scalar_tensor_tensor(out=t, in0=t, scalar=-0.5, in1=x, op0=ALU.mult, op1=ALU.mult))
                    then(V.scalar_tensor_tensor(out=y, in0=t, scalar=1.5, in1=y, op0=ALU.add, op1=ALU.mult))

            n = [0]

            def step(ins, settle=True):
                ins.then_inc(setup_steps, 1)
                n[0] += 1
                if settle:
                    dve.wait_ge(setup_steps, n[0])

            step(V.memset(rk[:, :, 0, :], 1.0), False)
            step(V.memset(dots[:], 0.0), False)
            step(V.memset(rdots[:], 0.0), False)
            step(V.memset(xf[:, :, D:D + 1], 1.0))
            dve.wait_ge(loaded, 16 * N_LOADS)
            step(V.tensor_scalar(sig, ids[:], 1.0 / 127.5, -1.0, ALU.mult, ALU.add))
            step(V.tensor_reduce(wmean, w1ext, AX, ALU.add))
            step(V.tensor_scalar(wmean, wmean, 1.0 / HID, None, ALU.mult))
            step(V.tensor_scalar(w1ext, w1ext, wmean, None, ALU.subtract))
            step(V.memset(cs, 1.0))
            dve.wait_ge(bins_summed, 1)
            step(V.tensor_copy(re_im, vec_ps[0:3 * BINS, 0:2 * ROWS]))
            re, im = re_im[:, 0:ROWS], re_im[:, ROWS:2 * ROWS]
            t0, t1, mag, zero, inv = tmp8
            step(V.tensor_tensor(t0, re, re, ALU.mult))
            step(V.tensor_tensor(t1, im, im, ALU.mult))
            step(V.tensor_tensor(t0, t0, t1, ALU.add))
            step(V.tensor_scalar(zero, t0, 0.0, None, ALU.is_equal))
            step(V.tensor_tensor(t1, t0, zero, ALU.add))
            rsqrt(step, inv, t1, mag)
            step(V.tensor_tensor(mag, t0, inv, ALU.mult))
            step(V.tensor_tensor(t0, re, inv, ALU.mult))
            step(V.tensor_tensor(cs[0:BINS], t0[0:BINS], zero[0:BINS], ALU.add))
            step(V.tensor_tensor(cs[BINS:2 * BINS], im[BINS:2 * BINS], inv[BINS:2 * BINS], ALU.mult))
            step(V.tensor_scalar(cs[2 * BINS:3 * BINS], mag[2 * BINS:3 * BINS], fb, None, ALU.mult))
            for b in range(ROWS):
                step(V.tensor_scalar(wb[:, b * HID:(b + 1) * HID], w1ext, cs[:, b:b + 1], None, ALU.mult))
            assert n[0] == SETUP_V, n

            with dve.Fori(0, NT) as t:
                dve.wait_ge(hid_squared, t + 1)
                a = stage("encode", t)
                a.then(V.tensor_reduce(rs_enc[0], sq_enc.rearrange("p (b n) -> p b n", b=ROWS), AX, ALU.add))
                a.then(V.tensor_scalar(rs_enc[1], rs_enc[0], 1.0 / HID, EPS, ALU.mult, ALU.add))
                rsqrt(a.then, rs_enc[0], rs_enc[1], rs_enc[2])
                for i in range(2):
                    r = rs_enc[0][:, 4 * i:4 * i + 4].unsqueeze(2).broadcast_to([P, 4, HID])
                    a.did(V.tensor_tensor(hn_enc[:, 512 * i:512 * i + 512].rearrange("p (b n) -> p b n", b=4),
                                          l1_ps[i][:].rearrange("p (b n) -> p b n", b=4), r, ALU.mult))
                a.close()
                dve.wait_ge(token_summed, t + 1)
                V.tensor_tensor(of_tile(t), vec_ps[:].rearrange("p (b d) -> p b d", b=ROWS),
                                b2e.unsqueeze(1).broadcast_to([P, ROWS, D]), ALU.add).then_inc(token_stored, 1)
            dve.wait_ge(token_stored, NT)

            def front(t):
                a = stage("front", t)
                norm(a, of_tile(t))
                a.did(V.tensor_tensor(sqr[:], cen[:], over_d(st[:, 3]), ALU.mult))
                a.then(V.tensor_tensor(st[:, 4], st[:, 2], st[:, 3], ALU.mult))
                a.then(V.tensor_tensor(st[:, 4], st[:, 4], st[:, 3], ALU.mult))
                a.then(V.tensor_scalar(st[:, 1], st[:, 4], EPS, None, ALU.add))
                rsqrt(a.then, st[:, 5], st[:, 1], st[:, 0])
                if not is_first(t):
                    dve.wait_ge(prj_full, fill(t - 2, EV_OT) + 1)
                a.did(V.tensor_tensor(onorm[:], sqr[:], over_d(st[:, 5]), ALU.mult))
                a.did(V.tensor_tensor(of_tile(t), of_tile(t), sqr[:], ALU.add))
                a.close()

            def mix(t):
                a = stage("mix", t)
                dve.wait_ge(prj_taken, fill(t - 1, EV_RV))
                a.did(V.tensor_scalar(be[:], be[:], 1.0, None, ALU.add))
                a.then(V.scalar_tensor_tensor(out=kq[:], in0=ex[:], scalar=1.0, in1=kq[:], op0=ALU.min, op1=ALU.add))
                a.did(V.reciprocal(br[:], be[:]))
                a.then(V.tensor_reduce(ksum[:], kq[:], AX, ALU.add))
                a.then(V.reciprocal(ik[:], ksum[:]))
                a.did(V.tensor_copy(mk[:, :, 1::2], ik[:, :, 1::2]))
                a.then(V.scalar_tensor_tensor(out=mk[:, :, 0::2], in0=ik[:, :, 0::2], scalar=-1.0,
                                              in1=br[:, :, 0, :].rearrange("p s h -> p h s"),
                                              op0=ALU.mult, op1=ALU.mult))
                a.close()

            def dot(a, lo, hi):
                for i in range(lo, hi):
                    m = 2 * ROWS - 1 - 2 * i
                    buf = prod if i % 2 == 0 else ex
                    a.then(V.tensor_tensor(buf[:, :, 0:m, :], kq[:, :, 2 * i + 1:, :],
                                           kq[:, :, 2 * i:2 * i + 1, :].broadcast_to([P, H, m, DH]), ALU.mult))
                    a.did(V.tensor_reduce(dots[:, :, i, 2 * i + 1:], buf[:, :, 0:m, :], AX, ALU.add))

            def scale_dots(a):
                a.settle()
                a.then(V.tensor_tensor(dots[:], dots[:], mk[:].unsqueeze(2).broadcast_to([P, H, ROWS, 2 * ROWS]), ALU.mult))
                a.then(V.tensor_tensor(dots[:], dots[:], ik[:, :, 0::2].unsqueeze(3).broadcast_to([P, H, ROWS, 2 * ROWS]),
                                       ALU.mult))
                a.close()

            def init(t):
                a = stage("init", t)
                dve.wait_ge(prj_taken, fill(t - 1, EVENTS))
                beta = [br[:, :, i, :].rearrange("p s h -> p h s").unsqueeze(3).broadcast_to([P, H, ROWS, DH])
                        for i in range(2)]
                a.did(V.tensor_tensor(acc[:, :, 0::2, :], v[:], beta[0], ALU.mult))
                a.then(V.tensor_tensor(ru[:], rv[:], beta[1], ALU.mult))
                a.close()

            def rk_prep(t):
                a = stage("rkprep", t)
                dve.wait_ge(prj_taken, fill(t, EV_RK + 3) + 1)
                a.then(V.tensor_reduce(rkm[:], rk[:, :, 1:, :], AX, ALU.max))
                a.did(V.tensor_tensor(rk[:, :, 1:, :], rk[:, :, 1:, :],
                                      rkm[:].unsqueeze(3).broadcast_to([P, H, ROWS, DH]), ALU.subtract))
                a.close()

            def rk_norm(t):
                a = stage("rknorm", t)
                dve.wait_ge(rk_exp, t + 1)
                a.then(V.tensor_reduce(rkm[:], rk[:, :, 1:, :], AX, ALU.add))
                a.then(V.reciprocal(rks[:], rkm[:]))
                a.then(V.tensor_tensor(rk[:, :, 1:, :], rk[:, :, 1:, :],
                                       rks[:].unsqueeze(3).broadcast_to([P, H, ROWS, DH]), ALU.mult))
                a.close()

            def r_dot(t):
                a = stage("rdots", t)
                a.did(V.tensor_scalar(nrb[:], br[:, :, 1, :].rearrange("p s h -> p h s"), -1.0, None, ALU.mult))
                for i in range(ROWS - 1):
                    m = ROWS - 1 - i
                    a.then(V.tensor_tensor(prod[:, :, 0:m, :], rk[:, :, i + 2:, :],
                                           rk[:, :, i + 1:i + 2, :].broadcast_to([P, H, m, DH]), ALU.mult))
                    a.then(V.tensor_reduce(rdots[:, :, i, i + 1:], prod[:, :, 0:m, :], AX, ALU.add))
                a.then(V.tensor_tensor(rdots[:], rdots[:], nrb[:].unsqueeze(2).broadcast_to([P, H, ROWS, ROWS]), ALU.mult))
                a.close()

            def delta(t):
                a = stage("delta", t)
                dve.wait_ge(z_cleared, t + 1)
                for i in range(ROWS):
                    m = 2 * ROWS - 1 - 2 * i
                    a.then(V.tensor_tensor(prod[:, :, 0:m, :],
                                           dots[:, :, i, 2 * i + 1:].unsqueeze(3).broadcast_to([P, H, m, DH]),
                                           acc[:, :, 2 * i:2 * i + 1, :].broadcast_to([P, H, m, DH]), ALU.mult))
                    a.then(V.tensor_tensor(acc[:, :, 2 * i + 1:, :], acc[:, :, 2 * i + 1:, :], prod[:, :, 0:m, :], ALU.add))
                a.close()

            def r_delta(t):
                a = stage("rdelta", t)
                for i in range(ROWS - 1):
                    m = ROWS - 1 - i
                    a.then(V.tensor_tensor(prod[:, :, 0:m, :],
                                           rdots[:, :, i, i + 1:].unsqueeze(3).broadcast_to([P, H, m, DH]),
                                           ru[:, :, i:i + 1, :].broadcast_to([P, H, m, DH]), ALU.mult))
                    a.then(V.tensor_tensor(ru[:, :, i + 1:, :], ru[:, :, i + 1:, :], prod[:, :, 0:m, :], ALU.add))
                a.close()

            def rec(t):
                a = stage("rec", t)
                if not is_first(t):
                    dve.wait_ge(prj_full, fill(t, EV_HST + 3) + 1)
                for i in range(ROWS):
                    m = i + 1
                    if i == 0:
                        a.then(V.tensor_reduce(qd[:, :, 1:2], rk[:, :, 1:2, :], AX, ALU.add))
                        a.then(V.tensor_scalar(qd[:, :, 1:2], qd[:, :, 1:2], 1.0 / DH, None, ALU.mult))
                    else:
                        dve.wait_ge(h_exp, t * (ROWS - 1) + i)
                        a.then(V.tensor_tensor(prod[:, :, 0:m + 1, :], rk[:, :, 0:m + 1, :],
                                               eh[:].unsqueeze(2).broadcast_to([P, H, m + 1, DH]), ALU.mult))
                        a.then(V.tensor_reduce(qd[:, :, 0:m + 1], prod[:, :, 0:m + 1, :], AX, ALU.add))
                        a.then(V.reciprocal(qr[:], qd[:, :, 0]))
                        a.then(V.tensor_tensor(qd[:, :, 1:m + 1], qd[:, :, 1:m + 1],
                                               qr[:].unsqueeze(2).broadcast_to([P, H, m]), ALU.mult))
                    a.then(V.tensor_tensor(prod[:, :, 0:m, :], ru[:, :, 0:m, :],
                                           qd[:, :, 1:m + 1].unsqueeze(3).broadcast_to([P, H, m, DH]), ALU.mult))
                    a.then(V.tensor_reduce(ht[:], prod[:, :, 0:m, :].rearrange("p h s d -> p h d s"), AX, ALU.add))
                    a.then(V.tensor_tensor(hs[:, i], ht[:], acc[:, :, 2 * i + 1, :], ALU.add))
                    if i < ROWS - 1:
                        a.then(V.tensor_reduce(hmax[:], hs[:, i], AX, ALU.max))
                        a.then(V.tensor_tensor(eh[:], hs[:, i], hmax[:].unsqueeze(2).broadcast_to([P, H, DH]), ALU.subtract))
                        assert a.n == REC_EXP(i)
                a.close()

            def back(t):
                a = stage("back", t)
                dve.wait_ge(vec_full, t * 3 + 1)
                a.then(V.tensor_tensor(hb[:], of_tile(t), vec_ps[:].rearrange("p (b d) -> p b d", b=ROWS), ALU.add))
                norm(a, hb[:])
                wait(dve, gx_ready, t * E)
                a.did(V.tensor_tensor(xf[:, :, 0:D], cen[:], over_d(st[:, 3]), ALU.mult))
                a.close()

            def gates(t):
                a = stage("gates", t)
                rk_bc = rank[:].unsqueeze(1).broadcast_to([P, ROWS, E])
                dve.wait_ge(vec_full, t * 3 + 2)
                a.then(V.tensor_tensor(lg[:, 0], vec_ps[:, 0:ROWS * E].rearrange("p (b e) -> p b e", b=ROWS),
                                       gate_b[:].unsqueeze(1).broadcast_to([P, ROWS, E]), ALU.add))
                for k, (src, m, one) in enumerate(((0, 0, 2), (1, 2, 4))):
                    a.then(V.tensor_reduce(gt[:, m], lg[:, src], AX, ALU.max))
                    a.then(V.tensor_tensor(lg[:, 5], lg[:, src], over_d(gt[:, m], E), ALU.is_equal))
                    a.then(V.tensor_tensor(lg[:, 5], lg[:, 5], rk_bc, ALU.mult))
                    a.then(V.tensor_reduce(gt[:, m + 1], lg[:, 5], AX, ALU.max))
                    a.then(V.tensor_tensor(lg[:, one], lg[:, 5], over_d(gt[:, m + 1], E), ALU.is_equal))
                    if k == 0:
                        a.then(V.scalar_tensor_tensor(out=lg[:, 1], in0=lg[:, 2], scalar=-BIG, in1=lg[:, 0],
                                                      op0=ALU.mult, op1=ALU.add))
                a.did(V.tensor_tensor(gt[:, 4], gt[:, 2], gt[:, 0], ALU.subtract))
                assert a.n == GATE_EXP

                dve.wait_ge(gate_exp, t + 1)
                a.then(V.tensor_scalar(gt[:, 6], gt[:, 5], 1.0, None, ALU.add))
                a.then(V.reciprocal(gt[:, 6], gt[:, 6]))
                a.did(V.tensor_tensor(lg[:, 3], lg[:, 2], over_d(gt[:, 6], E), ALU.mult))
                a.then(V.tensor_tensor(gt[:, 7], gt[:, 6], gt[:, 5], ALU.mult))
                a.then(V.tensor_tensor(lg[:, 5], lg[:, 4], over_d(gt[:, 7], E), ALU.mult))
                if not is_first(t):
                    dve.wait_ge(prj_full, fill(t, EV_GT) + 1)
                a.did(V.tensor_tensor(g[:], lg[:, 3], lg[:, 5], ALU.add))
                a.close()

            def tail(t):
                a = stage("tail", t)
                dve.wait_ge(vec_full, t * 3 + 3)
                a.then(V.tensor_tensor(cen[:], vec_ps[:].rearrange("p (b d) -> p b d", b=ROWS), xf[:, :, 0:D], ALU.add))
                norm(a, cen[:])
                a.then(V.tensor_tensor(sqr[:], cen[:], over_d(st[:, 3]), ALU.mult))
                a.then(V.tensor_tensor(sqr[:], sqr[:], gamb[:, 0, :].unsqueeze(1).broadcast_to([P, ROWS, D]), ALU.mult))
                a.then(V.tensor_tensor(sqr[:], sqr[:], gamb[:, 1, :].unsqueeze(1).broadcast_to([P, ROWS, D]), ALU.add))
                wait(dve, out_stored, t * 16)
                a.did(V.tensor_tensor(yo[:], sqr[:], hb[:], ALU.add))
                a.close()

            def iteration(t):
                if not (isinstance(t, int) and t == NT - 1):
                    front(t + 1)
                mix(t)
                if not is_first(t):
                    back(t - 1)
                rk_prep(t)
                a = stage("dots", t)
                dot(a, 0, 1)
                if not is_first(t):
                    gates(t - 1)
                dot(a, 1, ROWS)
                scale_dots(a)
                init(t)
                rk_norm(t)
                r_dot(t)
                delta(t)
                r_delta(t)
                rec(t)
                if not is_first(t):
                    tail(t - 1)

            front(0)
            iteration(0)
            iteration(1)
            with dve.Fori(2, NT - 1) as t:
                iteration(t)
            iteration(NT - 1)
            back(NT - 1)
            gates(NT - 1)
            tail(NT - 1)

        @block.tensor
        def _(pe):
            T_ = nc.tensor
            pe.wait_ge(loaded, 16 * N_LOADS)
            pe.wait_ge(setup_steps, 5)
            for part in range(2):
                for c in range(TC):
                    mm = T_.matmul(vec_ps[0:3 * BINS, part * ROWS:(part + 1) * ROWS],
                                   dft[:, c, part * 3 * BINS:(part + 1) * 3 * BINS], sig[:, :, c],
                                   start=(c == 0), stop=(c == TC - 1))
            mm.then_inc(bins_summed, 1)
            for c in range(SLOW_CHUNKS):
                wait(pe, slow_copied, c - 1)
                T_.transpose(prj_ps[c % 2][:, 0:SLOW_CHUNK], slow_raw[:, c].rearrange("p a d -> p (a d)"),
                             ident[0:SLOW_CHUNK, 0:SLOW_CHUNK]).then_inc(slow_turned, 1)
            pe.wait_ge(slow_copied, SLOW_CHUNKS)
            for c in range(2):
                mm = T_.transpose(prj_ps[0][:, c * D:(c + 1) * D], outw_raw[:, c * P:(c + 1) * P], ident[0:D, 0:D])
            mm.then_inc(outw_turned, 1)

            def hidden(t):
                pe.wait_ge(phase_copied, t + 1)
                wait(pe, v_did["encode"], t * STEPS["encode"])
                for i in range(2):
                    mm = T_.matmul(l1_ps[i][:], phase_now, wb[:, 512 * i:512 * i + 512], start=True, stop=True)
                mm.then_inc(hid_summed, 1)

            pe.wait_ge(setup_steps, SETUP_V)
            hidden(0)
            with pe.Fori(0, NT) as t:
                pe.wait_ge(v_did["encode"], t * STEPS["encode"] + STEPS["encode"])
                for b in range(ROWS):
                    mm = T_.transpose(y_ps[b // 4][:, (b % 4) * P:(b % 4 + 1) * P], hn_enc[:, b * P:(b + 1) * P], ident[:])
                mm.then_inc(hid_turned, 1)
                hidden(t + 1)
                pe.wait_ge(hid_gelu, t + 1)
                for b in range(ROWS):
                    mm = T_.matmul(vec_ps[:, b * D:(b + 1) * D], ge_enc[:, b * P:(b + 1) * P], w2e, start=True, stop=True)
                mm.then_inc(token_summed, 1)

            def event(t, ev, write):
                ps = prj_ps[parity(t, ev)]
                wait(pe, prj_taken, fill(t, ev) - 1)
                write(ps).then_inc(prj_full, 1)

            def project(ps, at, r, c0, n):
                half = (r % 2) * D
                return T_.matmul(ps[:, at:at + n], oT[half:half + D, r // 2, :], slowT[half:half + D, c0:c0 + n],
                                 start=True, stop=True)

            def o_turned(t):
                done(pe, "front", t + 1)

                def write(ps):
                    for c in range(ROWS // 2):
                        mm = T_.transpose(ps[:, c * P:(c + 1) * P],
                                          onorm[:, 2 * c:2 * c + 2, :].rearrange("p b d -> p (b d)"), ident[:])
                    return mm
                event(t - 1, EV_OT, write)
                pe.wait_ge(prj_taken, fill(t - 1, EV_OT) + 1)

            def kqv(t):
                for r in range(ROWS):
                    event(t - 1, EV_KQ + r, lambda ps: project(ps, 0, r, KQC, 2 * HD))
                for r in range(ROWS):
                    event(t - 1, EV_V + r, lambda ps: project(ps, 0, r, VC, HD + 2 * H))
                pair(t - 1, EV_RV, RVC)

            def pair(t, ev, c0):
                for i in range(ROWS // 2):
                    r = 4 * (i // 2) + i % 2

                    def write(ps):
                        project(ps, 0, r, c0, HD)
                        return project(ps, HD, r + 2, c0, HD)
                    event(t, ev + i, write)

            def h_turned(t):
                done(pe, "rec", t + 1)
                for i in range(4):
                    def write(ps):
                        for k in range(4):
                            r, c = 2 * i + k // 2, k % 2
                            mm = T_.transpose(ps[:, k * P:(k + 1) * P],
                                              hs[:, r, 4 * c:4 * c + 4, :].rearrange("p h d -> p (h d)"), ident[:])
                        return mm
                    event(t + 1, EV_HST + i, write)
                pe.wait_ge(prj_taken, fill(t + 1, EV_HST + 3) + 1)
                if is_first(t):
                    pe.wait_ge(token_stored, NT)
                else:
                    pe.wait_ge(v_did["tail"], (t - 1) * STEPS["tail"] + 1)
                for r in range(ROWS):
                    for c in range(2):
                        mm = T_.matmul(vec_ps[:, r * D:(r + 1) * D], hsT[:, 2 * r + c, :], outT[:, c, :],
                                       start=(c == 0), stop=(c == 1))
                mm.then_inc(vec_full, 1)

            def gate_logits(t):
                done(pe, "back", t + 1)
                for i in range(2):
                    def write(ps):
                        for k in range(4):
                            mm = T_.transpose(ps[0:D + 1, k * P:(k + 1) * P], xf[:, 4 * i + k, :], ident[:])
                        return mm
                    event(t + 1, EV_XFT + i, write)
                pe.wait_ge(prj_taken, fill(t + 1, EV_XFT + 1) + 1)
                for r in range(ROWS):
                    mm = T_.matmul(vec_ps[:, r * E:(r + 1) * E], xfT[:, r, :], gate_w[:], start=True, stop=True)
                mm.then_inc(vec_full, 1)
                done(pe, "gates", t + 1)
                event(t + 1, EV_GT, lambda ps: T_.transpose(ps[:, 0:P], g[:].rearrange("p b e -> p (b e)"), ident[:]))

            def experts(t, lo, hi):
                base = t * FFN_STEPS
                for slot in range(lo, hi):
                    if slot < FFN_STEPS:
                        e, grp = slot // GROUPS, slot % GROUPS
                        pe.wait_ge(gx_ready, t * E + (e + 1))
                        wait(pe, gxT_ready, base + slot)
                        for k in range(GROWS):
                            mm = T_.transpose(gx_ps[0:D + 1, k * P:(k + 1) * P], gx[e % GX_RING][:, GROWS * grp + k, :],
                                              ident[:])
                        mm.then_inc(gx_turned, 1)
                    k = slot - 1
                    if 0 <= k < FFN_STEPS:
                        pe.wait_ge(gxT_ready, base + (k + 1))
                        if k >= 2:
                            pe.wait_ge(hT_ready, base + (k - 1))
                        T_.matmul(l1_ps[k % 2][:], w1[:, k // GROUPS, :], gxT[k % 2][:], start=True,
                                  stop=True).then_inc(l1_done, 1)
                    k = slot - 2
                    if 0 <= k < FFN_STEPS:
                        e, grp = k // GROUPS, k % GROUPS
                        pe.wait_ge(hT_ready, base + (k + 1))
                        if e == 0:
                            wait(pe, y_copied, t)
                        mm = T_.matmul(y_ps[grp][0:D, :], w2[:, e, :], hT[k % 2][:], start=(e == 0), stop=(e == E - 1),
                                       skip_group_check=True)
                        mm.then_inc(l2_done, 1)
                        if e == 1:
                            if grp == 0:
                                if is_first(t):
                                    pe.wait_ge(b2_loaded, 16 * ROWS)
                                pe.wait_ge(prj_taken, fill(t + 1, EV_GT) + 1)
                            for q in range(GROWS):
                                T_.matmul(y_ps[grp][0:D, q * P:(q + 1) * P], b2rows[:, GROWS * grp + q, :], gT[:],
                                          start=False, stop=False, skip_group_check=True)

            def y_turned(t):
                pe.wait_ge(y_copied, t + 1)
                pe.wait_ge(v_did["gates"], t * STEPS["gates"] + 1)
                for r in range(ROWS):
                    mm = T_.matmul(vec_ps[:, r * D:(r + 1) * D], ysb[:, r, :], ident[0:D, 0:D], start=True, stop=True)
                mm.then_inc(vec_full, 1)

            def iteration(t):
                last = isinstance(t, int) and t == NT - 1
                if not is_first(t):
                    h_turned(t - 1)
                pair(t, EV_RK, RKC)
                if not is_first(t):
                    gate_logits(t - 1)
                if not last:
                    o_turned(t + 1)
                if not is_first(t):
                    experts(t - 1, 0, FFN_EARLY)
                if not last:
                    kqv(t + 1)
                if not is_first(t):
                    experts(t - 1, FFN_EARLY, FFN_SLOTS)
                    y_turned(t - 1)

            pe.wait_ge(slow_sorted, SORTS)
            o_turned(0)
            kqv(0)
            iteration(0)
            iteration(1)
            with pe.Fori(2, NT - 1) as t:
                iteration(t)
            iteration(NT - 1)
            h_turned(NT - 1)
            gate_logits(NT - 1)
            experts(NT - 1, 0, FFN_SLOTS)
            y_turned(NT - 1)

        @block.scalar
        def _(act):
            S = nc.scalar
            act.wait_ge(loaded, 16 * N_LOADS)
            for c in range(SLOW_CHUNKS):
                act.wait_ge(slow_turned, c + 1)
                S.copy(slowT_raw[:, c * SLOW_CHUNK:(c + 1) * SLOW_CHUNK], prj_ps[c % 2][:, 0:SLOW_CHUNK]).then_inc(slow_copied, 1)
            act.wait_ge(slow_copied, SLOW_CHUNKS)
            raw = slowT_raw.rearrange("p (h m) -> p h m", h=H)
            kqcols = slowT[:, KQC:KQC + 2 * HD].rearrange("p (h j d) -> p h j d", h=H, j=2)
            sorts = [(kqcols[:, :, 0, :], raw[:, :, DH:2 * DH]), (kqcols[:, :, 1, :], raw[:, :, 0:DH])]
            for c0, m0 in ((VC, 2 * DH), (RVC, 4 * DH), (RKC, 3 * DH)):
                sorts.append((slowT[:, c0:c0 + HD].rearrange("p (h d) -> p h d", h=H), raw[:, :, m0:m0 + DH]))
            for i in range(2):
                sorts.append((slowT[:, VC + HD + i * H:VC + HD + (i + 1) * H], raw[:, :, 5 * DH + i]))
            for dst, src in sorts:
                S.copy(dst, src).then_inc(slow_sorted, 1)
            act.wait_ge(outw_turned, 1)
            S.copy(outT[:].rearrange("p c d -> p (c d)"), prj_ps[0][:, 0:2 * D]).then_inc(slow_sorted, 1)
            assert len(sorts) + 1 == SORTS

            S.copy(phase_now, phase[:, 0:P]).then_inc(phase_copied, 1)
            with act.Fori(0, NT) as t:
                act.wait_ge(hid_summed, t + 1)
                for i in range(2):
                    q = S.activation(sq_enc[:, 512 * i:512 * i + 512], l1_ps[i][:], ACT.Square)
                q.then_inc(hid_squared, 1)
                S.copy(phase_now, phase[:, bass.ds((t + 1) * P, P)]).then_inc(phase_copied, 1)
                act.wait_ge(hid_turned, t + 1)
                for i in range(2):
                    q = S.activation(ge_enc[:, 512 * i:512 * i + 512], y_ps[i][:], ACT.Gelu, bias=bet_enc, scale=gam_enc)
                q.then_inc(hid_gelu, 1)
            act.wait_ge(phase_copied, NT + 1)
            act.wait_ge(hid_summed, NT + 1)
            act.wait_ge(token_stored, NT)

            def take(t, ev, copies):
                act.wait_ge(prj_full, fill(t, ev) + 1)
                q = None
                for f in copies(prj_ps[parity(t, ev)]):
                    q = f()
                q.then_inc(prj_taken, 1)

            def o_taken(t):
                take(t - 1, EV_OT, lambda ps: [lambda: S.activation(
                    oT[:].rearrange("p c n -> p (c n)"), ps[:], ACT.Identity, bias=lngb[:, 1:2], scale=lngb[:, 0:1])])

            def kqv_taken(t):
                done(act, "dots", t)
                for r in range(ROWS):
                    def copies(ps):
                        src = ps[:].rearrange("p (h j d) -> p h j d", h=H, j=2)
                        return [lambda: S.activation(ex[:, :, 2 * r:2 * r + 2, :], src, ACT.Exp),
                                lambda: S.activation(kq[:, :, 2 * r:2 * r + 2, :], src, ACT.Relu)]
                    take(t - 1, EV_KQ + r, copies)
                done(act, "init", t)
                for r in range(ROWS):
                    def copies(ps):
                        return [lambda: S.activation(be[:, r].rearrange("p a h -> p (a h)"), ps[:, HD:HD + 2 * H],
                                                     ACT.Exp, scale=-1.0),
                                lambda: S.copy(v[:, :, r, :], ps[:, 0:HD].rearrange("p (h d) -> p h d", h=H))]
                    take(t - 1, EV_V + r, copies)
                pair_taken(t - 1, EV_RV, rv, 0)

            def pair_taken(t, ev, dst, slot0):
                for i in range(ROWS // 2):
                    lo = slot0 + 4 * (i // 2) + i % 2
                    take(t, ev + i, lambda ps: [lambda: S.copy(
                        dst[:, :, lo:lo + 3:2, :].rearrange("p h s d -> p s h d"),
                        ps[:].rearrange("p (s h d) -> p s h d", s=2, h=H))])

            def rk_taken(t):
                done(act, "rec", t)
                pair_taken(t, EV_RK, rk, 1)

            def rk_exps(t):
                act.wait_ge(v_did["rkprep"], t * STEPS["rkprep"] + STEPS["rkprep"])
                S.activation(rk[:, :, 1:, :], rk[:, :, 1:, :], ACT.Exp).then_inc(rk_exp, 1)

            def h_taken(t):
                for i in range(4):
                    take(t + 1, EV_HST + i, lambda ps: [lambda: S.copy(
                        hsT[:, 4 * i:4 * i + 4, :].rearrange("p c n -> p (c n)"), ps[:])])

            def xf_taken(t):
                for i in range(2):
                    take(t + 1, EV_XFT + i, lambda ps: [lambda: S.copy(
                        xfT[:, 4 * i:4 * i + 4, :].rearrange("p c n -> p (c n)"), ps[0:D, :])])

            def gates_taken(t):
                act.wait_ge(v_did["gates"], t * STEPS["gates"] + GATE_EXP)
                S.activation(gt[:, 5], gt[:, 4], ACT.Exp).then_inc(gate_exp, 1)
                take(t + 1, EV_GT, lambda ps: [lambda: S.copy(gT[:], ps[:, 0:P])])

            def experts(t, lo, hi):
                base = t * FFN_STEPS
                for slot in range(lo, hi):
                    if slot < FFN_STEPS:
                        act.wait_ge(gx_turned, base + (slot + 1))
                        if slot >= 2:
                            act.wait_ge(l1_done, base + (slot - 1))
                        S.copy(gxT[slot % 2][:], gx_ps[0:D + 1, :]).then_inc(gxT_ready, 1)
                    k = slot - 1
                    if 0 <= k < FFN_STEPS:
                        act.wait_ge(l1_done, base + (k + 1))
                        if k >= 2:
                            act.wait_ge(l2_done, base + (k - 1))
                        S.activation(hT[k % 2][:], l1_ps[k % 2][:], ACT.Relu).then_inc(hT_ready, 1)

            def y_taken(t):
                act.wait_ge(l2_done, t * FFN_STEPS + FFN_STEPS)
                for i in range(2):
                    q = S.copy(ysb[:, 4 * i:4 * i + 4, :].rearrange("p r n -> p (r n)"), y_ps[i][0:D, :])
                q.then_inc(y_copied, 1)

            def iteration(t):
                last = isinstance(t, int) and t == NT - 1
                first = is_first(t)
                if not first:
                    h_taken(t - 1)
                rk_taken(t)
                if not first:
                    xf_taken(t - 1)
                rk_exps(t)
                if not first:
                    gates_taken(t - 1)
                if not last:
                    o_taken(t + 1)
                if not first:
                    experts(t - 1, 0, FFN_EARLY)
                if not last:
                    kqv_taken(t + 1)
                if not first:
                    experts(t - 1, FFN_EARLY, FFN_MID)
                for i in range(ROWS - 1):
                    act.wait_ge(v_did["rec"], t * STEPS["rec"] + REC_EXP(i))
                    S.activation(eh[:], eh[:], ACT.Exp).then_inc(h_exp, 1)
                    if not first:
                        experts(t - 1, FFN_MID + 2 * i, FFN_MID + 2 * i + 2)
                if not first:
                    y_taken(t - 1)

            act.wait_ge(slow_sorted, SORTS)
            o_taken(0)
            kqv_taken(0)
            iteration(0)
            iteration(1)
            with act.Fori(2, NT - 1) as t:
                iteration(t)
            iteration(NT - 1)
            h_taken(NT - 1)
            xf_taken(NT - 1)
            gates_taken(NT - 1)
            experts(NT - 1, 0, FFN_SLOTS)
            y_taken(NT - 1)


_INS = ["x", "L0_tok_freq_bands", "L0_tok_w1", "L0_tok_b1", "L0_tok_gamma", "L0_tok_beta", "L0_tok_w2", "L0_tok_b2",
        "L0_attn_slow_W", "L0_attn_out_W", "L0_attn_ln_g", "L0_attn_ln_b", "L0_ffn_gate_w", "L0_ffn_gate_b",
        "L0_ffn_w1", "L0_ffn_b1", "L0_ffn_w2", "L0_ffn_b2", "L0_ffn_gamma", "L0_ffn_beta"]


def _tables():
    import numpy as np

    two_pi = 2.0 * np.pi
    t, f = np.arange(T), np.arange(BINS)
    angle = two_pi * ((t[:, None] * f[None, :]) % T) / T
    cos, sin = np.cos(angle), np.sin(angle)
    dft = np.concatenate([cos, cos, cos, -sin, -sin, -sin], axis=1).reshape(P, TC, 6 * BINS)
    phase = np.zeros((FEATS, T + P))
    phase[0:BINS, 0:T] = sin.T
    phase[BINS:2 * BINS, 0:T] = cos.T
    phase[2 * BINS:, 0:T] = 1.0
    return {"dft": dft.astype(np.float32), "phase": phase.astype(np.float32), "ident": np.eye(P, dtype=np.float32),
            "rank": np.arange(E, 0, -1).astype(np.float32)}


def kernel(**inputs):
    import numpy as np
    import concourse.bacc as bacc
    from concourse.bass_utils import run_bass_kernel_spmd

    nc = bacc.Bacc("TRN2", target_bir_lowering=False, num_devices=1)
    named = {name: np.ascontiguousarray(inputs[name]) for name in _INS}
    named.update(_tables())
    arrays, args = {}, []
    for name, a in named.items():
        arrays[f"in_{name}"] = a
        args.append(nc.dram_tensor(f"in_{name}", a.shape, mybir.dt.from_np(a.dtype), kind="ExternalInput").ap())
    args.append(nc.dram_tensor("out_h", (ROWS, T, D), F32, kind="ExternalOutput").ap())
    build(nc, *args)
    r = run_bass_kernel_spmd(nc, [arrays], core_ids=[0])
    return r.results[0]["out_h"]
```

```python
from contextlib import ExitStack
from itertools import chain, islice

import concourse.bass as bass
from concourse import mybir

P = 128
ROWS, T = 8, 2048
NT = T // P
D = 64
BINS = 32
HID = 128
H, DH = 8, 32
HH = H // 2
H_EXPS = 2 * (ROWS - 1)
HD = H * DH
E, F = 16, 128
FEATS = 3 * BINS + 1
SLOW = H * (5 * DH + 2)
SLOW_CHUNK, SLOW_CHUNKS = 108, 12
EPS = 1e-5
RSQRT_SEED = float(0x5F3759DF)
NEWTON = 3
RSQRT = 2 + 3 * NEWTON
NORM = 7 + RSQRT
BIG = 3.0e38
TC = T // P
GROUPS = 2
GROWS = ROWS // GROUPS
FFN_STEPS = E * GROUPS
FFN_SLOTS = FFN_STEPS + 2
GX_RING = 3

F32 = mybir.dt.float32
I32 = mybir.dt.int32
ALU = mybir.AluOpType
ACT = mybir.ActivationFunctionType
AX = mybir.AxisListType.X

BACK1 = [("hsT", i) for i in range(ROWS // 2)]
BACK2 = [("xfT", 0), ("xfT", 1), ("gT", 0)]
NEXT = [("oT", 0)] + [("kq", i) for i in range(ROWS)]
VALUES = [[("v", i)] + [("rv", i // 2)] * (i % 2) for i in range(ROWS)]
OWN = [("rk", i) for i in range(ROWS // 2)]
FFN_TURNS = [("gx", i) for i in range(FFN_STEPS)]


def ring_order(back, own, ahead):
    return BACK1 * back + OWN * own + (BACK2 + FFN_TURNS) * back + (NEXT + sum(VALUES, [])) * ahead


FULL = ring_order(True, True, True)
RING = {-1: ring_order(False, False, True), 0: ring_order(False, True, True), NT - 1: ring_order(True, True, False),
        NT: ring_order(True, False, False)}


STEPS = dict(setup=20 + RSQRT + ROWS, encode=4 + RSQRT, front=NORM + 6 + RSQRT, mix=8, dots=17, rkprep=2, rksum=4, rdots=15,
             back=NORM + 2, gates=19, init=2, delta=14, rdelta=14, rec0=60, rec1=60, tail=NORM + 5)


def is_first(t):
    return isinstance(t, int) and t == 0


def fill(t, what, i=0):
    start = len(RING[-1]) + len(RING[0])
    if isinstance(t, int):
        start = {-1: 0, 0: len(RING[-1]), NT: start + len(FULL) * (NT - 2) + len(RING[NT - 1])}.get(
            t, start + len(FULL) * (t - 1))
        return start + RING.get(t, FULL).index((what, i))
    return t * len(FULL) + (start - len(FULL) + FULL.index((what, i)))


def parity(t, what, i=0):
    return fill(t if isinstance(t, int) else 2, what, i) % 2


class Stage:

    def __init__(self, eng, sem, name, tile):
        self.eng, self.sem, self.name, self.n = eng, sem, name, 0
        self.base = tile * STEPS[name]

    def did(self, ins):
        ins.then_inc(self.sem, 1)
        self.n += 1

    def settle(self):
        self.eng.wait_ge(self.sem, self.base + self.n)

    def then(self, ins):
        self.did(ins)
        self.settle()

    def close(self):
        self.settle()
        assert self.n == STEPS[self.name], (self.name, self.n)


FRONT_PER_MIX = 8
SMALL_PER_DOT = 1
TAIL_FROM = 30
GATE_EXP = 13
SORTS = 8


def REC_P2(i):
    return 4 + 8 * i


def REC_Z(i):
    return 1 if i == 0 else REC_P2(i - 1) + 1


def REC_EXP(i):
    return REC_P2(i) + 3


def wait(eng, sem, value):
    if not (isinstance(value, int) and value <= 0):
        eng.wait_ge(sem, value)


def build(nc, x, freq, tw1, tb1, tgam, tbet, tw2, tb2, slow, outw, lng, lnb, gw, gb, fw1, fb1, fw2, fb2,
          fgam, fbet, dft_d, phase_d, ident_d, rank_d, out):
    ctx = ExitStack()
    with ctx:
        def sb(name, shape, dt=F32):
            return ctx.enter_context(nc.sbuf_tensor(name, shape, dt))

        def sem(name):
            return ctx.enter_context(nc.semaphore(name))

        bank = [ctx.enter_context(nc.psum_tensor(f"bank{i}", [P, 512], F32)) for i in range(8)]
        vec_ps = bank[0]
        l1_ps = bank[1:3]
        h_ps = bank[3:5]
        ring_ps = bank[5:7]
        y_ps = bank[7]

        h_all = sb("h_all", [P, NT, ROWS, D])
        ident = sb("ident", [P, P])
        rank = sb("rank", [P, E])
        slowT = sb("slowT", [P, SLOW])
        KQC, VC, RVC, RKC = 0, 2 * HD, 3 * HD + 2 * H, 4 * HD + 2 * H
        outT = sb("outT", [P, 2, D])
        lngb = sb("lngb", [P, 2])
        gate_w = sb("gate_w", [D, E])
        gate_b = sb("gate_b", [P, E])
        w1 = sb("w1", [D + 1, E, F])
        w2 = sb("w2", [F, E, D])
        b2rows = sb("b2rows", [P, ROWS, D])
        gamb = sb("gamb", [P, 2, D])

        kq = sb("kq", [P, H, 2 * ROWS, DH])
        ex = sb("ex", [P, H, 2 * ROWS, DH])
        prod = sb("prod", [P, H, 2 * ROWS, DH])
        u = sb("u", [P, H, ROWS, DH])
        zprod = sb("zprod", [P, H, ROWS, DH])
        v = sb("v", [P, H, ROWS, DH])
        rv = sb("rv", [P, H, ROWS, DH])
        rk = sb("rk", [P, H, ROWS + 1, DH])
        ru = sb("ru", [P, H, ROWS, DH])
        hs = sb("hs", [P, ROWS, H, DH])
        hsT = ru[:].rearrange("p h s d -> p (h s d)").rearrange("p (c n) -> p c n", c=2 * ROWS)
        rprod = hs[:].rearrange("p s h d -> p (s h d)").rearrange("p (h s d) -> p h s d", h=H, s=ROWS)
        dots = sb("dots", [P, H, ROWS, 2 * ROWS])
        rdots = sb("rdots", [P, H, ROWS, ROWS])
        be = sb("be", [P, ROWS, 2, H])
        br = sb("br", [P, ROWS, 2, H])
        ksum = sb("ksum", [P, H, 2 * ROWS])
        ik = sb("ik", [P, H, 2 * ROWS])
        mk = sb("mk", [P, H, 2 * ROWS])
        rkm = sb("rkm", [P, H, ROWS])
        rks = sb("rks", [P, H, ROWS])
        ub = sb("ub", [P, H, ROWS])
        rub = sb("rub", [P, H, ROWS])
        nrb = sb("nrb", [P, H, ROWS])
        eh = sb("eh", [P, H, DH])
        qd = sb("qd", [P, H, ROWS + 1])
        qr = sb("qr", [P, H])
        hmax = sb("hmax", [P, H])

        cen = sb("cen", [P, ROWS, D])
        sqr = sb("sqr", [P, ROWS, D])
        onorm = sb("onorm", [P, ROWS, D])
        oT = sb("oT", [P, ROWS // 2, P])
        st = sb("st", [P, 8, ROWS])
        hb = sb("hb", [P, ROWS, D])
        xf = sb("xf", [P, ROWS, D + 1])
        xfT = sb("xfT", [D, ROWS, P])
        lg = sb("lg", [P, 6, ROWS, E])
        gt = sb("gt", [P, 8, ROWS])
        g = sb("g", [P, ROWS, E])
        gT = sb("gT", [P, P])
        gx = [sb(f"gx{i}", [P, ROWS, D + 1]) for i in range(GX_RING)]
        gxT = [sb(f"gxT{i}", [D + 1, 512]) for i in range(2)]
        hT = [sb(f"hT{i}", [F, 512]) for i in range(2)]
        ysb = sb("ysb", [P, 512])
        yo = sb("yo", [P, ROWS, D])

        phase = ex[0:FEATS].rearrange("p h s d -> p (h s d)")[:, 0:T + P]
        phase_now = hs[0:FEATS].rearrange("p s h d -> p (s h d)")[:, 0:P]
        flat_v = v[:].rearrange("p h s d -> p (h s d)")
        flat_rv = rv[:].rearrange("p h s d -> p (h s d)")
        flat_ru = ru[:].rearrange("p h s d -> p (h s d)")
        flat_kq = kq[:].rearrange("p h s d -> p (h s d)")
        flat_prod = prod[:].rearrange("p h s d -> p (h s d)")
        flat_u = u[:].rearrange("p h s d -> p (h s d)")
        dft = flat_prod[:, 0:TC * 2 * 3 * BINS].rearrange("p (c n) -> p c n", c=TC)
        wb = flat_kq[0:FEATS, 0:ROWS * HID]
        sq_enc = flat_kq[:, 1024:2048]
        hn_enc = flat_kq[:, 2048:3072]
        ge_enc = flat_kq[:, 3072:4096]
        w1ext = flat_rv[0:FEATS, 0:HID]
        w2e = flat_rv[:, 128:192]
        b2e = flat_rv[:, 192:256]
        cs = flat_rv[0:FEATS, 256:264]
        fb = flat_rv[2 * BINS:3 * BINS, 264:265]
        gam_enc = flat_rv[:, 265:266]
        bet_enc = flat_rv[:, 266:267]
        wmean = flat_rv[0:FEATS, 267:268]
        re_im = flat_rv[0:3 * BINS, 272:288]
        tmp8 = [flat_rv[0:3 * BINS, 288 + 8 * i:296 + 8 * i] for i in range(5)]
        rs_enc = [flat_rv[:, 336 + 8 * i:344 + 8 * i] for i in range(3)]
        sig = flat_rv[:, 384:512].rearrange("p (b c) -> p b c", b=ROWS)
        ids = flat_rv[:, 512:512 + ROWS * TC].bitcast(I32).rearrange("p (b c) -> p b c", b=ROWS)
        slow_raw = flat_u[0:SLOW_CHUNK, 0:SLOW_CHUNKS * 2 * D].rearrange("p (c a d) -> p c a d", c=SLOW_CHUNKS, a=2)
        slowT_raw = flat_ru[:, 0:SLOW]
        outw_raw = flat_v[0:D, 0:HD]

        loaded = sem("loaded")
        b2_cleared = sem("b2_cleared")
        b2_loaded = sem("b2_loaded")
        setup_steps = sem("setup_steps")
        bins_summed = sem("bins_summed")
        bins_copied = sem("bins_copied")
        slow_turned = sem("slow_turned")
        slow_copied = sem("slow_copied")
        slow_sorted = sem("slow_sorted")
        outw_turned = sem("outw_turned")
        phase_copied = sem("phase_copied")
        hid_summed = sem("hid_summed")
        hid_squared = sem("hid_squared")
        hid_turned = sem("hid_turned")
        hid_gelu = sem("hid_gelu")
        token_summed = sem("token_summed")
        token_stored = sem("token_stored")
        v_did = {name: sem("v_" + name) for name in STEPS if name != "setup"}
        ring_full = sem("ring_full")
        ring_taken = sem("ring_taken")
        vec_full = sem("vec_full")
        rk_exp = sem("rk_exp")
        h_exp = sem("h_exp")
        gate_exp = sem("gate_exp")
        gx_ready = sem("gx_ready")
        l1_done = sem("l1_done")
        hT_ready = sem("hT_ready")
        l2_done = sem("l2_done")
        y_copied = sem("y_copied")
        z_summed = [sem(f"z_summed{i}") for i in range(2)]
        h_summed = [sem(f"h_summed{i}") for i in range(2)]
        hs_copied = [sem(f"hs_copied{i}") for i in range(2)]
        out_stored = sem("out_stored")

        block = ctx.enter_context(nc.Block())
        N_LOADS = 28

        def row(a):
            return a.rearrange("(a n) -> a n", a=1)

        def col(a):
            return a.rearrange("(n a) -> n a", a=1)

        def of_tile(t):
            return h_all[:, bass.ds(t, 1)].rearrange("p a b d -> p (a b) d")

        def done(eng, stage, tiles):
            for name in ("rec0", "rec1") if stage == "rec" else (stage,):
                wait(eng, v_did[name], tiles * STEPS[name])

        @block.sync
        def _(sp):
            n = [0]

            def load(dst, src):
                sp.dma_start(dst, src).then_inc(loaded, 16)
                n[0] += 1

            load(ids, x.rearrange("b (p c) -> p b c", c=TC))
            load(dft, dft_d)
            load(w1ext[0:BINS], tw1[BINS:2 * BINS, :])
            load(w1ext[BINS:2 * BINS], tw1[BINS:2 * BINS, :])
            load(w1ext[2 * BINS:3 * BINS], tw1[0:BINS, :])
            load(w1ext[3 * BINS:FEATS], row(tb1))
            load(fb, col(freq))
            load(phase, phase_d)
            load(ident[:], ident_d)
            load(gam_enc, col(tgam))
            load(bet_enc, col(tbet))
            load(w2e, tw2)
            load(b2e, row(tb2).broadcast_to([P, D]))
            load(slow_raw[:, :, 0, :], slow.rearrange("(c p) d -> p c d", p=SLOW_CHUNK))
            load(slow_raw[:, :, 1, :], slow.rearrange("(c p) d -> p c d", p=SLOW_CHUNK))
            load(outw_raw, outw)
            for half in (0, D):
                load(lngb[half:half + D, 0:1], col(lng))
                load(lngb[half:half + D, 1:2], col(lnb))
            load(rank[:], row(rank_d).broadcast_to([P, E]))
            load(gate_w[:], gw)
            load(gate_b[:], row(gb).broadcast_to([P, E]))
            load(w1[0:D], fw1.rearrange("e h f -> h e f"))
            load(w1[D:D + 1], fb1.unsqueeze(0))
            load(w2[:], fw2.rearrange("e f h -> f e h"))
            load(gamb[:, 0, :], row(fgam).broadcast_to([P, D]))
            load(gamb[:, 1, :], row(fbet).broadcast_to([P, D]))
            assert n[0] == N_LOADS, n
            sp.wait_ge(b2_cleared, 1)
            for r in range(ROWS):
                sp.dma_start(b2rows[r * E:(r + 1) * E, r, :], fb2).then_inc(b2_loaded, 16)

            with sp.Fori(0, NT) as t:
                sp.wait_ge(v_did["tail"], t * STEPS["tail"] + STEPS["tail"])
                sp.dma_start(out[:, bass.ds(t * P, P), :].rearrange("b p d -> p b d"), yo[:]).then_inc(out_stored, 16)
            sp.wait_ge(out_stored, 16 * NT)

        @block.gpsimd
        def _(pool):
            pool.memset(b2rows[:], 0.0).then_inc(b2_cleared, 1)

            def gate_inputs(t):
                done(pool, "gates", t + 1)
                for e in range(E):
                    if e >= GX_RING:
                        pool.wait_ge(ring_full, fill(t + 1, "gx", GROUPS * (e - GX_RING + 1) - 1) + 1)
                    elif not is_first(t):
                        pool.wait_ge(ring_full, fill(t, "gx", GROUPS * (E + e - GX_RING + 1) - 1) + 1)
                    pool.tensor_tensor(gx[e % GX_RING][:], xf[:],
                                       g[:, :, e:e + 1].broadcast_to([P, ROWS, D + 1]), ALU.mult).then_inc(gx_ready, 1)

            gate_inputs(0)
            with pool.Fori(1, NT - 2) as t:
                gate_inputs(t)
            gate_inputs(NT - 2)
            gate_inputs(NT - 1)

        @block.vector
        def _(dve):
            V = nc.vector

            def stage(name, t):
                return Stage(dve, v_did[name], name, t)

            def over_d(y, n=D):
                return y.unsqueeze(2).broadcast_to([P, ROWS, n])

            def run(steps):
                for _ in steps:
                    pass

            def weave(main, side, n):
                for _ in main:
                    for _ in range(n):
                        next(side, None)

            def norm(a, src):
                a.did(V.tensor_reduce(st[:, 0], src, AX, ALU.add))
                yield
                a.settle()
                a.did(V.tensor_scalar(st[:, 1], st[:, 0], 1.0 / D, None, ALU.mult))
                yield
                a.settle()
                a.did(V.tensor_tensor(cen[:], src, over_d(st[:, 1]), ALU.subtract))
                yield
                a.settle()
                a.did(V.tensor_tensor(sqr[:], cen[:], cen[:], ALU.mult))
                yield
                a.settle()
                a.did(V.tensor_reduce(st[:, 0], sqr[:], AX, ALU.add))
                yield
                a.settle()
                a.did(V.tensor_scalar(st[:, 2], st[:, 0], 1.0 / D, None, ALU.mult))
                yield
                a.settle()
                a.did(V.tensor_scalar(st[:, 1], st[:, 2], EPS, None, ALU.add))
                yield
                a.settle()
                yield from rsqrt(a, st[:, 3], st[:, 1], st[:, 0])

            def rsqrt(a, y, x, t):
                a.did(V.tensor_scalar(t.bitcast(I32), x.bitcast(I32), 1, None, ALU.logical_shift_right))
                yield
                a.settle()
                a.did(V.tensor_scalar(y.bitcast(I32), t.bitcast(I32), -1.0, RSQRT_SEED, ALU.mult, ALU.add))
                yield
                a.settle()
                for _ in range(NEWTON):
                    a.did(V.tensor_tensor(t, y, y, ALU.mult))
                    yield
                    a.settle()
                    a.did(V.scalar_tensor_tensor(out=t, in0=t, scalar=-0.5, in1=x, op0=ALU.mult, op1=ALU.mult))
                    yield
                    a.settle()
                    a.did(V.scalar_tensor_tensor(out=y, in0=t, scalar=1.5, in1=y, op0=ALU.add, op1=ALU.mult))
                    yield
                    a.settle()

            a = Stage(dve, setup_steps, "setup", 0)
            a.did(V.memset(rk[:, :, 0, :], 1.0))
            a.did(V.memset(dots[:], 0.0))
            a.did(V.memset(rdots[:], 0.0))
            a.did(V.memset(xf[:, :, D:D + 1], 1.0))
            dve.wait_ge(loaded, 16 * N_LOADS)
            a.then(V.tensor_scalar(sig, ids, 1.0 / 127.5, -1.0, ALU.mult, ALU.add))
            a.then(V.tensor_reduce(wmean, w1ext, AX, ALU.add))
            a.then(V.tensor_scalar(wmean, wmean, 1.0 / HID, None, ALU.mult))
            a.then(V.tensor_scalar(w1ext, w1ext, wmean, None, ALU.subtract))
            a.then(V.memset(cs, 1.0))
            dve.wait_ge(bins_summed, 1)
            a.then(V.tensor_copy(re_im, vec_ps[0:3 * BINS, 0:2 * ROWS]))
            re, im = re_im[:, 0:ROWS], re_im[:, ROWS:2 * ROWS]
            t0, t1, mag, zero, inv = tmp8
            a.then(V.tensor_tensor(t0, re, re, ALU.mult))
            a.then(V.tensor_tensor(t1, im, im, ALU.mult))
            a.then(V.tensor_tensor(t0, t0, t1, ALU.add))
            a.then(V.tensor_scalar(zero, t0, 0.0, None, ALU.is_equal))
            a.then(V.tensor_tensor(t1, t0, zero, ALU.add))
            run(rsqrt(a, inv, t1, mag))
            a.then(V.tensor_tensor(mag, t0, inv, ALU.mult))
            a.then(V.tensor_tensor(t0, re, inv, ALU.mult))
            a.then(V.tensor_tensor(cs[0:BINS], t0[0:BINS], zero[0:BINS], ALU.add))
            a.then(V.tensor_tensor(cs[BINS:2 * BINS], im[BINS:2 * BINS], inv[BINS:2 * BINS], ALU.mult))
            a.then(V.tensor_scalar(cs[2 * BINS:3 * BINS], mag[2 * BINS:3 * BINS], fb, None, ALU.mult))
            for b in range(ROWS):
                a.then(V.tensor_scalar(wb[:, b * HID:(b + 1) * HID], w1ext, cs[:, b:b + 1], None, ALU.mult))
            a.close()

            with dve.Fori(0, NT) as t:
                dve.wait_ge(hid_squared, t + 1)
                a = stage("encode", t)
                a.then(V.tensor_reduce(rs_enc[0], sq_enc.rearrange("p (b n) -> p b n", b=ROWS), AX, ALU.add))
                a.then(V.tensor_scalar(rs_enc[1], rs_enc[0], 1.0 / HID, EPS, ALU.mult, ALU.add))
                run(rsqrt(a, rs_enc[0], rs_enc[1], rs_enc[2]))
                for i in range(2):
                    r = rs_enc[0][:, 4 * i:4 * i + 4].unsqueeze(2).broadcast_to([P, 4, HID])
                    a.did(V.tensor_tensor(hn_enc[:, 512 * i:512 * i + 512].rearrange("p (b n) -> p b n", b=4),
                                          l1_ps[i][:].rearrange("p (b n) -> p b n", b=4), r, ALU.mult))
                a.close()
                dve.wait_ge(token_summed, t + 1)
                V.tensor_tensor(of_tile(t), vec_ps[:].rearrange("p (b d) -> p b d", b=ROWS),
                                b2e.unsqueeze(1).broadcast_to([P, ROWS, D]), ALU.add).then_inc(token_stored, 1)
            dve.wait_ge(token_stored, NT)

            def front(t):
                a = stage("front", t)
                yield from norm(a, of_tile(t))
                a.did(V.tensor_tensor(sqr[:], cen[:], over_d(st[:, 3]), ALU.mult))
                a.did(V.tensor_tensor(st[:, 4], st[:, 2], st[:, 3], ALU.mult))
                yield
                a.settle()
                a.did(V.tensor_tensor(st[:, 4], st[:, 4], st[:, 3], ALU.mult))
                yield
                a.settle()
                a.did(V.tensor_scalar(st[:, 1], st[:, 4], EPS, None, ALU.add))
                yield
                a.settle()
                yield from rsqrt(a, st[:, 5], st[:, 1], st[:, 0])
                if not is_first(t):
                    dve.wait_ge(ring_full, fill(t - 2, "oT") + 1)
                a.did(V.tensor_tensor(onorm[:], sqr[:], over_d(st[:, 5]), ALU.mult))
                a.did(V.tensor_tensor(of_tile(t), of_tile(t), sqr[:], ALU.add))
                a.close()

            def mix(t):
                a = stage("mix", t)
                dve.wait_ge(ring_taken, fill(t - 1, "v", ROWS - 1) + 1)
                a.did(V.tensor_scalar(be[:], be[:], 1.0, None, ALU.add))
                a.did(V.scalar_tensor_tensor(out=kq[:], in0=ex[:], scalar=1.0, in1=kq[:], op0=ALU.min, op1=ALU.add))
                yield
                a.settle()
                a.did(V.reciprocal(br[:], be[:]))
                a.did(V.tensor_reduce(ksum[:], kq[:], AX, ALU.add))
                yield
                a.settle()
                a.did(V.reciprocal(ik[:], ksum[:]))
                yield
                a.settle()
                beta = br[:, :, 0, :].rearrange("p s h -> p h s")
                a.did(V.tensor_copy(mk[:, :, 1::2], ik[:, :, 1::2]))
                a.did(V.tensor_tensor(ub[:], ik[:, :, 0::2], beta, ALU.mult))
                yield
                a.settle()
                a.did(V.scalar_tensor_tensor(out=mk[:, :, 0::2], in0=ub[:], scalar=-1.0, in1=ik[:, :, 0::2],
                                             op0=ALU.mult, op1=ALU.mult))
                yield
                a.close()

            def dot(t):
                a = stage("dots", t)
                for half in range(2):
                    wait(dve, h_summed[half], t * ROWS)
                for i in range(ROWS):
                    m = 2 * ROWS - 1 - 2 * i
                    buf = prod if i % 2 == 0 else ex
                    a.did(V.tensor_tensor(buf[:, :, 0:m, :], kq[:, :, 2 * i + 1:, :],
                                          kq[:, :, 2 * i:2 * i + 1, :].broadcast_to([P, H, m, DH]), ALU.mult))
                    yield
                    a.settle()
                    a.did(V.tensor_reduce(dots[:, :, i, 2 * i + 1:], buf[:, :, 0:m, :], AX, ALU.add))
                    yield
                a.settle()
                a.did(V.tensor_tensor(dots[:], dots[:], mk[:].unsqueeze(2).broadcast_to([P, H, ROWS, 2 * ROWS]), ALU.mult))
                yield
                a.close()

            def init(t):
                a = stage("init", t)
                dve.wait_ge(ring_taken, fill(t - 1, "rv", ROWS // 2 - 1) + 1)
                a.did(V.tensor_tensor(u[:], v[:], ub[:].unsqueeze(3).broadcast_to([P, H, ROWS, DH]), ALU.mult))
                yield
                a.did(V.tensor_tensor(ru[:], rv[:], rub[:].unsqueeze(3).broadcast_to([P, H, ROWS, DH]), ALU.mult))
                yield
                a.close()

            def rk_prep(t):
                a = stage("rkprep", t)
                dve.wait_ge(ring_taken, fill(t, "rk", ROWS // 2 - 1) + 1)
                a.did(V.tensor_reduce(rkm[:], rk[:, :, 1:, :], AX, ALU.max))
                yield
                a.settle()
                a.did(V.tensor_tensor(rk[:, :, 1:, :], rk[:, :, 1:, :],
                                      rkm[:].unsqueeze(3).broadcast_to([P, H, ROWS, DH]), ALU.subtract))
                a.close()

            def rk_sum(t):
                a = stage("rksum", t)
                dve.wait_ge(rk_exp, t + 1)
                a.did(V.tensor_reduce(rkm[:], rk[:, :, 1:, :], AX, ALU.add))
                yield
                a.settle()
                a.did(V.reciprocal(rks[:], rkm[:]))
                yield
                a.settle()
                a.did(V.tensor_tensor(rub[:], rks[:], br[:, :, 1, :].rearrange("p s h -> p h s"), ALU.mult))
                yield
                a.settle()
                a.did(V.scalar_tensor_tensor(out=nrb[:], in0=rub[:], scalar=-1.0, in1=rks[:], op0=ALU.mult, op1=ALU.mult))
                yield
                a.close()

            def r_dot(t):
                a = stage("rdots", t)
                if not is_first(t):
                    dve.wait_ge(ring_full, fill(t, "hsT", ROWS // 2 - 1) + 1)
                for i in range(ROWS - 1):
                    m = ROWS - 1 - i
                    a.did(V.tensor_tensor(rprod[:, :, 0:m, :], rk[:, :, i + 2:, :],
                                           rk[:, :, i + 1:i + 2, :].broadcast_to([P, H, m, DH]), ALU.mult))
                    yield
                    a.settle()
                    a.did(V.tensor_reduce(rdots[:, :, i, i + 1:], rprod[:, :, 0:m, :], AX, ALU.add))
                    yield
                    a.settle()
                a.did(V.tensor_tensor(rdots[:], rdots[:], nrb[:].unsqueeze(2).broadcast_to([P, H, ROWS, ROWS]), ALU.mult))
                yield
                a.settle()
                a.close()

            def delta(t):
                a = stage("delta", t)
                for i in range(ROWS - 1):
                    m = ROWS - 1 - i
                    a.did(V.tensor_tensor(prod[:, :, 0:m, :],
                                          dots[:, :, i, 2 * i + 2::2].unsqueeze(3).broadcast_to([P, H, m, DH]),
                                          u[:, :, i:i + 1, :].broadcast_to([P, H, m, DH]), ALU.mult))
                    yield
                    a.settle()
                    a.did(V.tensor_tensor(u[:, :, i + 1:, :], u[:, :, i + 1:, :], prod[:, :, 0:m, :], ALU.add))
                    yield
                    a.settle()
                a.close()

            def r_delta(t):
                a = stage("rdelta", t)
                for i in range(ROWS - 1):
                    m = ROWS - 1 - i
                    a.did(V.tensor_tensor(rprod[:, :, 0:m, :],
                                           rdots[:, :, i, i + 1:].unsqueeze(3).broadcast_to([P, H, m, DH]),
                                           ru[:, :, i:i + 1, :].broadcast_to([P, H, m, DH]), ALU.mult))
                    yield
                    a.settle()
                    a.did(V.tensor_tensor(ru[:, :, i + 1:, :], ru[:, :, i + 1:, :], rprod[:, :, 0:m, :], ALU.add))
                    yield
                    a.settle()
                a.close()

            def rec(t, half):
                a = stage(f"rec{half}", t)
                hh = slice(half * HH, (half + 1) * HH)
                p_, qd_, qr_, eh_, hmax_ = prod[:, hh], qd[:, hh], qr[:, hh], eh[:, hh], hmax[:, hh]
                h_sum = h_ps[half][:, 0:HH * DH].rearrange("p (h d) -> p h d", h=HH)

                def z_products(i):
                    m = i + 1
                    wait(dve, z_summed[half], t * ROWS + i)
                    a.did(V.tensor_tensor(zprod[:, hh, 0:m, :],
                                          dots[:, hh, 0:m, 2 * i + 1].unsqueeze(3).broadcast_to([P, HH, m, DH]),
                                          u[:, hh, 0:m, :], ALU.mult))
                    assert a.n == REC_Z(i)

                z_products(0)
                yield
                for i in range(ROWS):
                    m = i + 1
                    if i == 0:
                        a.did(V.tensor_reduce(qd_[:, :, 1:2], rk[:, hh, 1:2, :], AX, ALU.add))
                        yield
                        a.settle()
                        a.did(V.tensor_scalar(qd_[:, :, 1:2], qd_[:, :, 1:2], 1.0 / DH, None, ALU.mult))
                        yield
                        a.settle()
                    else:
                        dve.wait_ge(h_exp, t * H_EXPS + (2 * (i - 1) + half + 1))
                        a.did(V.tensor_tensor(p_[:, :, 0:m + 1, :], rk[:, hh, 0:m + 1, :],
                                              eh_.unsqueeze(2).broadcast_to([P, HH, m + 1, DH]), ALU.mult))
                        yield
                        a.settle()
                        a.did(V.tensor_reduce(qd_[:, :, 0:m + 1], p_[:, :, 0:m + 1, :], AX, ALU.add))
                        yield
                        a.settle()
                        a.did(V.reciprocal(qr_, qd_[:, :, 0]))
                        yield
                        a.settle()
                        a.did(V.tensor_tensor(qd_[:, :, 1:m + 1], qd_[:, :, 1:m + 1],
                                              qr_.unsqueeze(2).broadcast_to([P, HH, m]), ALU.mult))
                        yield
                        a.settle()
                    a.did(V.tensor_tensor(p_[:, :, 0:m, :], ru[:, hh, 0:m, :],
                                          qd_[:, :, 1:m + 1].unsqueeze(3).broadcast_to([P, HH, m, DH]), ALU.mult))
                    assert a.n == REC_P2(i)
                    yield
                    if i < ROWS - 1:
                        z_products(i + 1)
                        yield
                        dve.wait_ge(h_summed[half], t * ROWS + (i + 1))
                        a.did(V.tensor_reduce(hmax_, h_sum, AX, ALU.max))
                        yield
                        a.settle()
                        a.did(V.tensor_tensor(eh_, h_sum, hmax_.unsqueeze(2).broadcast_to([P, HH, DH]), ALU.subtract))
                        assert a.n == REC_EXP(i)
                        yield
                a.close()

            def back(t):
                a = stage("back", t)
                dve.wait_ge(vec_full, t * 3 + 1)
                a.did(V.tensor_tensor(hb[:], of_tile(t), vec_ps[:].rearrange("p (b d) -> p b d", b=ROWS), ALU.add))
                yield
                a.settle()
                yield from norm(a, hb[:])
                wait(dve, gx_ready, t * E)
                a.did(V.tensor_tensor(xf[:, :, 0:D], cen[:], over_d(st[:, 3]), ALU.mult))
                a.close()

            def gates(t):
                a = stage("gates", t)
                rk_bc = rank[:].unsqueeze(1).broadcast_to([P, ROWS, E])
                dve.wait_ge(vec_full, t * 3 + 2)
                a.did(V.tensor_tensor(lg[:, 0], vec_ps[:, 0:ROWS * E].rearrange("p (b e) -> p b e", b=ROWS),
                                       gate_b[:].unsqueeze(1).broadcast_to([P, ROWS, E]), ALU.add))
                yield
                a.settle()
                for k, (src, m, one) in enumerate(((0, 0, 2), (1, 2, 4))):
                    a.did(V.tensor_reduce(gt[:, m], lg[:, src], AX, ALU.max))
                    yield
                    a.settle()
                    a.did(V.tensor_tensor(lg[:, 5], lg[:, src], over_d(gt[:, m], E), ALU.is_equal))
                    yield
                    a.settle()
                    a.did(V.tensor_tensor(lg[:, 5], lg[:, 5], rk_bc, ALU.mult))
                    yield
                    a.settle()
                    a.did(V.tensor_reduce(gt[:, m + 1], lg[:, 5], AX, ALU.max))
                    yield
                    a.settle()
                    a.did(V.tensor_tensor(lg[:, one], lg[:, 5], over_d(gt[:, m + 1], E), ALU.is_equal))
                    yield
                    a.settle()
                    if k == 0:
                        a.did(V.scalar_tensor_tensor(out=lg[:, 1], in0=lg[:, 2], scalar=-BIG, in1=lg[:, 0],
                                                      op0=ALU.mult, op1=ALU.add))
                        yield
                        a.settle()
                a.did(V.tensor_tensor(gt[:, 4], gt[:, 2], gt[:, 0], ALU.subtract))
                assert a.n == GATE_EXP

                dve.wait_ge(gate_exp, t + 1)
                a.did(V.tensor_scalar(gt[:, 6], gt[:, 5], 1.0, None, ALU.add))
                yield
                a.settle()
                a.did(V.reciprocal(gt[:, 6], gt[:, 6]))
                yield
                a.settle()
                a.did(V.tensor_tensor(lg[:, 3], lg[:, 2], over_d(gt[:, 6], E), ALU.mult))
                a.did(V.tensor_tensor(gt[:, 7], gt[:, 6], gt[:, 5], ALU.mult))
                yield
                a.settle()
                a.did(V.tensor_tensor(lg[:, 5], lg[:, 4], over_d(gt[:, 7], E), ALU.mult))
                yield
                a.settle()
                if not is_first(t):
                    dve.wait_ge(ring_full, fill(t, "gT") + 1)
                a.did(V.tensor_tensor(g[:], lg[:, 3], lg[:, 5], ALU.add))
                a.close()

            def tail(t):
                a = stage("tail", t)
                dve.wait_ge(vec_full, t * 3 + 3)
                a.did(V.tensor_tensor(cen[:], vec_ps[:].rearrange("p (b d) -> p b d", b=ROWS), xf[:, :, 0:D], ALU.add))
                yield
                a.settle()
                yield from norm(a, cen[:])
                a.did(V.tensor_tensor(sqr[:], cen[:], over_d(st[:, 3]), ALU.mult))
                yield
                a.settle()
                a.did(V.tensor_tensor(sqr[:], sqr[:], gamb[:, 0, :].unsqueeze(1).broadcast_to([P, ROWS, D]), ALU.mult))
                yield
                a.settle()
                a.did(V.tensor_tensor(sqr[:], sqr[:], gamb[:, 1, :].unsqueeze(1).broadcast_to([P, ROWS, D]), ALU.add))
                yield
                a.settle()
                wait(dve, out_stored, t * 16)
                a.did(V.tensor_tensor(yo[:], sqr[:], hb[:], ALU.add))
                a.close()

            def iteration(t):
                first, last = is_first(t), isinstance(t, int) and t == NT - 1
                weave(mix(t), iter(()) if last else front(t + 1), FRONT_PER_MIX)
                before = iter(()) if first else back(t - 1)
                weave(rk_prep(t), before, 12)
                run(before)
                dotting = dot(t)
                next(dotting)
                gating = iter(()) if first else gates(t - 1)
                weave(islice(dotting, 2), gating, 9)
                run(gating)
                small = chain(rk_sum(t), init(t), r_dot(t), r_delta(t))
                weave(dotting, small, SMALL_PER_DOT)
                weave(delta(t), small, 1)
                run(small)
                halves = rec(t, 0), rec(t, 1)
                end = tail(t - 1) if not first else iter(())
                for k, _ in enumerate(halves[0]):
                    next(halves[1], None)
                    if k >= TAIL_FROM:
                        next(end, None)
                run(halves[1])
                run(end)

            run(front(0))
            iteration(0)
            iteration(1)
            with dve.Fori(2, NT - 1) as t:
                iteration(t)
            iteration(NT - 1)
            run(back(NT - 1))
            run(gates(NT - 1))
            run(tail(NT - 1))

        @block.tensor
        def _(pe):
            T_ = nc.tensor
            pe.wait_ge(loaded, 16 * N_LOADS)
            pe.wait_ge(setup_steps, 5)
            for part in range(2):
                for c in range(TC):
                    mm = T_.matmul(vec_ps[0:3 * BINS, part * ROWS:(part + 1) * ROWS],
                                   dft[:, c, part * 3 * BINS:(part + 1) * 3 * BINS], sig[:, :, c],
                                   start=(c == 0), stop=(c == TC - 1))
            mm.then_inc(bins_summed, 1)
            for c in range(SLOW_CHUNKS):
                wait(pe, slow_copied, c - 1)
                T_.transpose(ring_ps[c % 2][:, 0:SLOW_CHUNK], slow_raw[:, c].rearrange("p a d -> p (a d)"),
                             ident[0:SLOW_CHUNK, 0:SLOW_CHUNK]).then_inc(slow_turned, 1)
            pe.wait_ge(slow_copied, SLOW_CHUNKS)
            for c in range(2):
                mm = T_.transpose(ring_ps[0][:, c * D:(c + 1) * D], outw_raw[:, c * P:(c + 1) * P], ident[0:D, 0:D])
            mm.then_inc(outw_turned, 1)

            def hidden(t):
                pe.wait_ge(phase_copied, t + 1)
                wait(pe, v_did["encode"], t * STEPS["encode"])
                for i in range(2):
                    mm = T_.matmul(l1_ps[i][:], phase_now, wb[:, 512 * i:512 * i + 512], start=True, stop=True)
                mm.then_inc(hid_summed, 1)

            pe.wait_ge(setup_steps, STEPS["setup"])
            hidden(0)
            with pe.Fori(0, NT) as t:
                pe.wait_ge(v_did["encode"], t * STEPS["encode"] + STEPS["encode"])
                for b in range(ROWS):
                    mm = T_.transpose(h_ps[b // 4][:, (b % 4) * P:(b % 4 + 1) * P], hn_enc[:, b * P:(b + 1) * P], ident[:])
                mm.then_inc(hid_turned, 1)
                hidden(t + 1)
                pe.wait_ge(hid_gelu, t + 1)
                for b in range(ROWS):
                    mm = T_.matmul(vec_ps[:, b * D:(b + 1) * D], ge_enc[:, b * P:(b + 1) * P], w2e, start=True, stop=True)
                mm.then_inc(token_summed, 1)

            def event(t, what, i, write):
                wait(pe, ring_taken, fill(t, what, i) - 1)
                write(ring_ps[parity(t, what, i)]).then_inc(ring_full, 1)

            def project(ps, at, r, c0, n):
                half = (r % 2) * D
                return T_.matmul(ps[:, at:at + n], oT[half:half + D, r // 2, :], slowT[half:half + D, c0:c0 + n],
                                 start=True, stop=True)

            def o_turned(t):
                done(pe, "front", t + 1)

                def write(ps):
                    for c in range(ROWS // 2):
                        mm = T_.transpose(ps[:, c * P:(c + 1) * P],
                                          onorm[:, 2 * c:2 * c + 2, :].rearrange("p b d -> p (b d)"), ident[:])
                    return mm
                event(t - 1, "oT", 0, write)
                pe.wait_ge(ring_taken, fill(t - 1, "oT") + 1)

            def kq_projected(t):
                for r in range(ROWS):
                    event(t - 1, "kq", r, lambda ps: project(ps, 0, r, KQC, 2 * HD))

            def values_projected(t, i):
                event(t - 1, "v", i, lambda ps: project(ps, 0, i, VC, HD + 2 * H))
                if i % 2:
                    pair(t - 1, "rv", i // 2, RVC)

            def pair(t, what, i, c0):
                r = 4 * (i // 2) + i % 2

                def write(ps):
                    project(ps, 0, r, c0, HD)
                    return project(ps, HD, r + 2, c0, HD)
                event(t, what, i, write)

            def h_turned(t):
                for i in range(ROWS // 2):
                    for half in range(2):
                        pe.wait_ge(hs_copied[half], t * ROWS + (2 * i + 2))

                    def write(ps):
                        for k in range(4):
                            r, c = 2 * i + k // 2, k % 2
                            mm = T_.transpose(ps[:, k * P:(k + 1) * P],
                                              hs[:, r, 4 * c:4 * c + 4, :].rearrange("p h d -> p (h d)"), ident[:])
                        return mm
                    event(t + 1, "hsT", i, write)
                pe.wait_ge(ring_taken, fill(t + 1, "hsT", ROWS // 2 - 1) + 1)
                if is_first(t):
                    pe.wait_ge(token_stored, NT)
                else:
                    pe.wait_ge(v_did["tail"], (t - 1) * STEPS["tail"] + 1)
                for r in range(ROWS):
                    for c in range(2):
                        mm = T_.matmul(vec_ps[:, r * D:(r + 1) * D], hsT[:, 2 * r + c, :], outT[:, c, :],
                                       start=(c == 0), stop=(c == 1))
                mm.then_inc(vec_full, 1)

            def gate_logits(t):
                done(pe, "back", t + 1)
                for i in range(2):
                    def write(ps):
                        for k in range(4):
                            mm = T_.transpose(ps[0:D + 1, k * P:(k + 1) * P], xf[:, 4 * i + k, :], ident[:])
                        return mm
                    event(t + 1, "xfT", i, write)
                pe.wait_ge(ring_taken, fill(t + 1, "xfT", 1) + 1)
                for r in range(ROWS):
                    mm = T_.matmul(vec_ps[:, r * E:(r + 1) * E], xfT[:, r, :], gate_w[:], start=True, stop=True)
                mm.then_inc(vec_full, 1)
                done(pe, "gates", t + 1)
                event(t + 1, "gT", 0, lambda ps: T_.transpose(ps[:, 0:P], g[:].rearrange("p b e -> p (b e)"), ident[:]))

            def recurrence(t, last):
                def summed(half, src, m, last):
                    for j in range(m):
                        mm = T_.matmul(h_ps[half][:, 0:HH * DH], ident[:], src[:, half * HH:(half + 1) * HH, j, :],
                                       start=(j == 0 and not last), stop=(j == m - 1 and last), skip_group_check=True)
                    return mm

                for i in range(ROWS):
                    for half in range(2):
                        pe.wait_ge(v_did[f"rec{half}"], t * STEPS[f"rec{half}"] + REC_Z(i))
                        wait(pe, hs_copied[half], t * ROWS + i)
                        summed(half, zprod, i + 1, False).then_inc(z_summed[half], 1)
                    for half in range(2):
                        pe.wait_ge(v_did[f"rec{half}"], t * STEPS[f"rec{half}"] + REC_P2(i))
                        summed(half, prod, i + 1, True).then_inc(h_summed[half], 1)
                    if not last:
                        values_projected(t + 1, i)

            def experts(t):
                base = t * FFN_STEPS
                for slot in range(FFN_SLOTS):
                    if slot < FFN_STEPS:
                        e, grp = slot // GROUPS, slot % GROUPS
                        pe.wait_ge(gx_ready, t * E + (e + 1))

                        def write(ps):
                            for k in range(GROWS):
                                mm = T_.transpose(ps[0:D + 1, k * P:(k + 1) * P],
                                                  gx[e % GX_RING][:, GROWS * grp + k, :], ident[:])
                            return mm
                        event(t + 1, "gx", slot, write)
                    k = slot - 1
                    if 0 <= k < FFN_STEPS:
                        pe.wait_ge(ring_taken, fill(t + 1, "gx", k) + 1)
                        if k >= 2:
                            pe.wait_ge(hT_ready, base + (k - 1))
                        T_.matmul(l1_ps[k % 2][:], w1[:, k // GROUPS, :], gxT[k % 2][:], start=True,
                                  stop=True).then_inc(l1_done, 1)
                    k = slot - 2
                    if 0 <= k < FFN_STEPS:
                        e, grp = k // GROUPS, k % GROUPS
                        part = slice(grp * D, (grp + 1) * D)
                        pe.wait_ge(hT_ready, base + (k + 1))
                        if e == 0:
                            wait(pe, y_copied, t)
                        T_.matmul(y_ps[part, :], w2[:, e, :], hT[k % 2][:], start=(e == 0), stop=(e == E - 1),
                                  skip_group_check=True).then_inc(l2_done, 1)
                        if e == 1:
                            if grp == 0:
                                if is_first(t):
                                    pe.wait_ge(b2_loaded, 16 * ROWS)
                                pe.wait_ge(ring_taken, fill(t + 1, "gT") + 1)
                            for q in range(GROWS):
                                T_.matmul(y_ps[part, q * P:(q + 1) * P], b2rows[:, GROWS * grp + q, :], gT[:],
                                          start=False, stop=False, skip_group_check=True)

            def y_turned(t):
                pe.wait_ge(y_copied, t + 1)
                pe.wait_ge(v_did["gates"], t * STEPS["gates"] + 1)
                for q in range(GROWS):
                    mm = T_.transpose(vec_ps[:].rearrange("p (a q d) -> p q a d", a=GROUPS, q=GROWS)[:, q],
                                      ysb[:, q * P:(q + 1) * P], ident[:])
                mm.then_inc(vec_full, 1)

            def iteration(t):
                first, last = is_first(t), isinstance(t, int) and t == NT - 1
                if not first:
                    h_turned(t - 1)
                for i in range(ROWS // 2):
                    pair(t, "rk", i, RKC)
                if not first:
                    gate_logits(t - 1)
                    experts(t - 1)
                if not last:
                    o_turned(t + 1)
                    kq_projected(t + 1)
                if not first:
                    y_turned(t - 1)
                recurrence(t, last)

            pe.wait_ge(slow_sorted, SORTS)
            o_turned(0)
            kq_projected(0)
            for i in range(ROWS):
                values_projected(0, i)
            iteration(0)
            iteration(1)
            with pe.Fori(2, NT - 1) as t:
                iteration(t)
            iteration(NT - 1)
            h_turned(NT - 1)
            gate_logits(NT - 1)
            experts(NT - 1)
            y_turned(NT - 1)

        @block.scalar
        def _(act):
            S = nc.scalar
            act.wait_ge(loaded, 16 * N_LOADS)
            for c in range(SLOW_CHUNKS):
                act.wait_ge(slow_turned, c + 1)
                S.copy(slowT_raw[:, c * SLOW_CHUNK:(c + 1) * SLOW_CHUNK], ring_ps[c % 2][:, 0:SLOW_CHUNK]).then_inc(slow_copied, 1)
            act.wait_ge(slow_copied, SLOW_CHUNKS)
            raw = slowT_raw.rearrange("p (h m) -> p h m", h=H)
            kqcols = slowT[:, KQC:KQC + 2 * HD].rearrange("p (h j d) -> p h j d", h=H, j=2)
            sorts = [(kqcols[:, :, 0, :], raw[:, :, DH:2 * DH]), (kqcols[:, :, 1, :], raw[:, :, 0:DH])]
            for c0, m0 in ((VC, 2 * DH), (RVC, 4 * DH), (RKC, 3 * DH)):
                sorts.append((slowT[:, c0:c0 + HD].rearrange("p (h d) -> p h d", h=H), raw[:, :, m0:m0 + DH]))
            for i in range(2):
                sorts.append((slowT[:, VC + HD + i * H:VC + HD + (i + 1) * H], raw[:, :, 5 * DH + i]))
            for dst, src in sorts:
                S.copy(dst, src).then_inc(slow_sorted, 1)
            act.wait_ge(outw_turned, 1)
            S.copy(outT[:].rearrange("p c d -> p (c d)"), ring_ps[0][:, 0:2 * D]).then_inc(slow_sorted, 1)
            assert len(sorts) + 1 == SORTS

            S.copy(phase_now, phase[:, 0:P]).then_inc(phase_copied, 1)
            with act.Fori(0, NT) as t:
                act.wait_ge(hid_summed, t + 1)
                for i in range(2):
                    q = S.activation(sq_enc[:, 512 * i:512 * i + 512], l1_ps[i][:], ACT.Square)
                q.then_inc(hid_squared, 1)
                S.copy(phase_now, phase[:, bass.ds((t + 1) * P, P)]).then_inc(phase_copied, 1)
                act.wait_ge(hid_turned, t + 1)
                for i in range(2):
                    q = S.activation(ge_enc[:, 512 * i:512 * i + 512], h_ps[i][:], ACT.Gelu, bias=bet_enc, scale=gam_enc)
                q.then_inc(hid_gelu, 1)
            act.wait_ge(phase_copied, NT + 1)
            act.wait_ge(hid_summed, NT + 1)
            act.wait_ge(token_stored, NT)

            def take(t, what, i, copies):
                act.wait_ge(ring_full, fill(t, what, i) + 1)
                q = None
                for f in copies(ring_ps[parity(t, what, i)]):
                    q = f()
                q.then_inc(ring_taken, 1)

            def o_taken(t):
                take(t - 1, "oT", 0, lambda ps: [lambda: S.activation(
                    oT[:].rearrange("p c n -> p (c n)"), ps[:], ACT.Identity, bias=lngb[:, 1:2], scale=lngb[:, 0:1])])

            def kq_taken(t):
                done(act, "dots", t)
                for r in range(ROWS):
                    def copies(ps):
                        src = ps[:].rearrange("p (h j d) -> p h j d", h=H, j=2)
                        return [lambda: S.activation(ex[:, :, 2 * r:2 * r + 2, :], src, ACT.Exp),
                                lambda: S.activation(kq[:, :, 2 * r:2 * r + 2, :], src, ACT.Relu)]
                    take(t - 1, "kq", r, copies)
                done(act, "init", t)

            def values_taken(t, r):
                def copies(ps):
                    return [lambda: S.activation(be[:, r].rearrange("p a h -> p (a h)"), ps[:, HD:HD + 2 * H],
                                                 ACT.Exp, scale=-1.0),
                            lambda: S.copy(v[:, :, r, :], ps[:, 0:HD].rearrange("p (h d) -> p h d", h=H))]
                take(t - 1, "v", r, copies)
                if r % 2:
                    pair_taken(t - 1, "rv", r // 2, rv, 0)

            def pair_taken(t, what, i, dst, slot0):
                lo = slot0 + 4 * (i // 2) + i % 2
                take(t, what, i, lambda ps: [lambda: S.copy(
                    dst[:, :, lo:lo + 3:2, :].rearrange("p h s d -> p s h d"),
                    ps[:].rearrange("p (s h d) -> p s h d", s=2, h=H))])

            def rk_taken(t):
                done(act, "rec", t)
                for i in range(ROWS // 2):
                    pair_taken(t, "rk", i, rk, 1)

            def rk_exps(t):
                act.wait_ge(v_did["rkprep"], t * STEPS["rkprep"] + STEPS["rkprep"])
                S.activation(rk[:, :, 1:, :], rk[:, :, 1:, :], ACT.Exp).then_inc(rk_exp, 1)

            def h_taken(t):
                for i in range(ROWS // 2):
                    take(t + 1, "hsT", i, lambda ps: [lambda: S.copy(
                        hsT[:, 4 * i:4 * i + 4, :].rearrange("p c n -> p (c n)"), ps[:])])

            def xf_taken(t):
                for i in range(2):
                    take(t + 1, "xfT", i, lambda ps: [lambda: S.copy(
                        xfT[:, 4 * i:4 * i + 4, :].rearrange("p c n -> p (c n)"), ps[0:D, :])])

            def gates_taken(t):
                act.wait_ge(v_did["gates"], t * STEPS["gates"] + GATE_EXP)
                S.activation(gt[:, 5], gt[:, 4], ACT.Exp).then_inc(gate_exp, 1)
                take(t + 1, "gT", 0, lambda ps: [lambda: S.copy(gT[:], ps[:, 0:P])])

            def experts(t):
                base = t * FFN_STEPS
                for slot in range(FFN_SLOTS):
                    if slot < FFN_STEPS:
                        if slot >= 2:
                            act.wait_ge(l1_done, base + (slot - 1))
                        take(t + 1, "gx", slot, lambda ps: [lambda: S.copy(gxT[slot % 2][:], ps[0:D + 1, :])])
                    k = slot - 1
                    if 0 <= k < FFN_STEPS:
                        act.wait_ge(l1_done, base + (k + 1))
                        if k >= 2:
                            act.wait_ge(l2_done, base + (k - 1))
                        S.activation(hT[k % 2][:], l1_ps[k % 2][:], ACT.Relu).then_inc(hT_ready, 1)

            def y_taken(t):
                act.wait_ge(l2_done, t * FFN_STEPS + FFN_STEPS)
                S.copy(ysb[:], y_ps[:]).then_inc(y_copied, 1)

            def iteration(t):
                last = isinstance(t, int) and t == NT - 1
                first = is_first(t)
                if not first:
                    h_taken(t - 1)
                rk_taken(t)
                if not first:
                    xf_taken(t - 1)
                rk_exps(t)
                if not first:
                    gates_taken(t - 1)
                if not first:
                    experts(t - 1)
                    y_taken(t - 1)
                if not last:
                    o_taken(t + 1)
                    kq_taken(t + 1)
                for i in range(ROWS):
                    for half in range(2):
                        if i < ROWS - 1:
                            act.wait_ge(v_did[f"rec{half}"], t * STEPS[f"rec{half}"] + REC_EXP(i))
                            part = eh[:, half * HH:(half + 1) * HH]
                            S.activation(part, part, ACT.Exp).then_inc(h_exp, 1)
                        else:
                            act.wait_ge(h_summed[half], t * ROWS + ROWS)
                        S.copy(hs[:, i, half * HH:(half + 1) * HH],
                               h_ps[half][:, 0:HH * DH].rearrange("p (h d) -> p h d", h=HH)).then_inc(hs_copied[half], 1)
                    if not last:
                        values_taken(t + 1, i)

            act.wait_ge(slow_sorted, SORTS)
            o_taken(0)
            kq_taken(0)
            for i in range(ROWS):
                values_taken(0, i)
            iteration(0)
            iteration(1)
            with act.Fori(2, NT - 1) as t:
                iteration(t)
            iteration(NT - 1)
            h_taken(NT - 1)
            xf_taken(NT - 1)
            gates_taken(NT - 1)
            experts(NT - 1)
            y_taken(NT - 1)


_INS = ["x", "L0_tok_freq_bands", "L0_tok_w1", "L0_tok_b1", "L0_tok_gamma", "L0_tok_beta", "L0_tok_w2", "L0_tok_b2",
        "L0_attn_slow_W", "L0_attn_out_W", "L0_attn_ln_g", "L0_attn_ln_b", "L0_ffn_gate_w", "L0_ffn_gate_b",
        "L0_ffn_w1", "L0_ffn_b1", "L0_ffn_w2", "L0_ffn_b2", "L0_ffn_gamma", "L0_ffn_beta"]


def _tables():
    import numpy as np

    two_pi = 2.0 * np.pi
    t, f = np.arange(T), np.arange(BINS)
    angle = two_pi * ((t[:, None] * f[None, :]) % T) / T
    cos, sin = np.cos(angle), np.sin(angle)
    dft = np.concatenate([cos, cos, cos, -sin, -sin, -sin], axis=1).reshape(P, TC, 6 * BINS)
    phase = np.zeros((FEATS, T + P))
    phase[0:BINS, 0:T] = sin.T
    phase[BINS:2 * BINS, 0:T] = cos.T
    phase[2 * BINS:, 0:T] = 1.0
    return {"dft": dft.astype(np.float32), "phase": phase.astype(np.float32), "ident": np.eye(P, dtype=np.float32),
            "rank": np.arange(E, 0, -1).astype(np.float32)}


def kernel(**inputs):
    import numpy as np
    import concourse.bacc as bacc
    from concourse.bass_utils import run_bass_kernel_spmd

    nc = bacc.Bacc("TRN2", target_bir_lowering=False, num_devices=1)
    named = {name: np.ascontiguousarray(inputs[name]) for name in _INS}
    named.update(_tables())
    arrays, args = {}, []
    for name, a in named.items():
        arrays[f"in_{name}"] = a
        args.append(nc.dram_tensor(f"in_{name}", a.shape, mybir.dt.from_np(a.dtype), kind="ExternalInput").ap())
    args.append(nc.dram_tensor("out_h", (ROWS, T, D), F32, kind="ExternalOutput").ap())
    build(nc, *args)
    r = run_bass_kernel_spmd(nc, [arrays], core_ids=[0])
    return r.results[0]["out_h"]
```

```python
from contextlib import ExitStack
from itertools import chain, islice

import concourse.bass as bass
from concourse import mybir

P = 128
ROWS, T = 8, 2048
NT = T // P
D = 64
BINS = 32
HID = 128
H, DH = 8, 32
HH = H // 2
H_EXPS = 2 * (ROWS - 1)
HD = H * DH
E, F = 16, 128
FEATS = 3 * BINS + 1
SLOW = H * (5 * DH + 2)
SLOW_CHUNK, SLOW_CHUNKS = 108, 12
EPS = 1e-5
RSQRT_SEED = float(0x5F3759DF)
NEWTON = 3
RSQRT = 2 + 3 * NEWTON
NORM = 7 + RSQRT
BIG = 3.0e38
TC = T // P
GROUPS = 2
GROWS = ROWS // GROUPS
FFN_STEPS = E * GROUPS
PAIRS = NT // 2
PARTS = 4
FFN_SLOTS = FFN_STEPS + 2
GX_RING = 3

F32 = mybir.dt.float32
I32 = mybir.dt.int32
ALU = mybir.AluOpType
ACT = mybir.ActivationFunctionType
AX = mybir.AxisListType.X

BACK1 = [("hsT", i) for i in range(ROWS // 2)]
BACK2 = [("xfT", 0), ("xfT", 1), ("gT", 0)]
BESIDE = [[],
          [("v", 0)],
          [("kq", 0), ("v", 1)],
          [("kq", 1), ("kq", 2), ("rv", 0)],
          [("kq", 3), ("kq", 4), ("v", 2), ("v", 3)],
          [("kq", 5), ("kq", 6), ("v", 4), ("rv", 1)],
          [("kq", 7), ("v", 5), ("v", 6), ("rv", 2)],
          [("v", 7), ("rv", 3)]]
SLOTS_BESIDE = [1, 1, 1, 1, 0, 0, 0, 0]
FFN_BEFORE = FFN_SLOTS - sum(SLOTS_BESIDE)


def slots_beside(i):
    lo = FFN_BEFORE + sum(SLOTS_BESIDE[:i])
    return lo, lo + SLOTS_BESIDE[i]


OWN = [("rk", i) for i in range(ROWS // 2)]
FFN_TURNS = [("gx", i) for i in range(FFN_STEPS)]


def ring_order(back, own, ahead):
    order = BACK1 * back + OWN * own + (BACK2 + FFN_TURNS[:FFN_BEFORE]) * back + [("oT", 0)] * ahead
    for i in range(ROWS):
        lo, hi = slots_beside(i)
        order += BESIDE[i] * ahead + FFN_TURNS[lo:hi] * back
    return order


FULL = ring_order(True, True, True)
assert len(FULL) % 2 == 0
RING = {-1: ring_order(False, False, True), 0: ring_order(False, True, True), NT - 1: ring_order(True, True, False),
        NT: ring_order(True, False, False)}


STEPS = dict(setup=20 + RSQRT + ROWS, encode=9 + RSQRT, front=NORM + 6 + RSQRT, mix=8, dots=17, rkprep=2, rksum=4, rdots=15,
             back=NORM + 2, gates=19, init=2, delta=14, rdelta=13, rec0=74, rec1=74, tail=NORM + 5)


def is_first(t):
    return isinstance(t, int) and t == 0


def fill(t, what, i=0):
    start = len(RING[-1]) + len(RING[0])
    if isinstance(t, int):
        start = {-1: 0, 0: len(RING[-1]), NT: start + len(FULL) * (NT - 2) + len(RING[NT - 1])}.get(
            t, start + len(FULL) * (t - 1))
        return start + RING.get(t, FULL).index((what, i))
    return t * len(FULL) + (start - len(FULL) + FULL.index((what, i)))


def parity(t, what, i=0):
    return fill(t if isinstance(t, int) else 2, what, i) % 2


class Stage:

    def __init__(self, eng, sem, name, tile):
        self.eng, self.sem, self.name, self.n = eng, sem, name, 0
        self.base = tile * STEPS[name]

    def did(self, ins):
        ins.then_inc(self.sem, 1)
        self.n += 1

    def settle(self):
        self.eng.wait_ge(self.sem, self.base + self.n)

    def then(self, ins):
        self.did(ins)
        self.settle()

    def close(self):
        self.settle()
        assert self.n == STEPS[self.name], (self.name, self.n)


MIX_BEFORE_BACK = 2
BACK_PER_MIX = 10
GATES_PER_DOT = 9
SMALL_PER_DOT = 1
Y_ROW = 4
TAIL_FROM = 48
GATE_EXP = 13
SORTS = 8


def REC_P2(i):
    return 4 + 10 * i


def REC_Z(i):
    return 1 if i == 0 else REC_P2(i - 1) + 1


def REC_EXP(i):
    return REC_P2(i) + 3


def wait(eng, sem, value):
    if not (isinstance(value, int) and value <= 0):
        eng.wait_ge(sem, value)


def build(nc, x, freq, tw1, tb1, tgam, tbet, tw2, tb2, slow, outw, lng, lnb, gw, gb, fw1, fb1, fw2, fb2,
          fgam, fbet, dft_d, phase_d, ident_d, rank_d, out):
    ctx = ExitStack()
    with ctx:
        def sb(name, shape, dt=F32):
            return ctx.enter_context(nc.sbuf_tensor(name, shape, dt))

        def sem(name):
            return ctx.enter_context(nc.semaphore(name))

        bank = [ctx.enter_context(nc.psum_tensor(f"bank{i}", [P, 512], F32)) for i in range(8)]
        vec_ps = bank[0]
        l1_ps = bank[1:3]
        h_ps = bank[3:5]
        ring_ps = bank[5:7]
        y_ps = bank[7]
        token_ps = [vec_ps, y_ps]

        h_all = sb("h_all", [P, NT, ROWS, D])
        ident = sb("ident", [P, P])
        rank = sb("rank", [P, E])
        slowT = sb("slowT", [P, SLOW])
        KQC, VC, RVC, RKC = 0, 2 * HD, 3 * HD + 2 * H, 4 * HD + 2 * H
        outT = sb("outT", [P, 2, D])
        lngb = sb("lngb", [P, 2])
        gate_w = sb("gate_w", [D, E])
        gate_b = sb("gate_b", [P, E])
        w1 = sb("w1", [D + 1, E, F])
        w2 = sb("w2", [F, E, D])
        b2rows = sb("b2rows", [P, ROWS, D])
        gamb = sb("gamb", [P, 2, D])

        kq = sb("kq", [P, H, 2 * ROWS, DH])
        ex = sb("ex", [P, H, 2 * ROWS, DH])
        prod = sb("prod", [P, H, 2 * ROWS, DH])
        u = sb("u", [P, H, ROWS, DH])
        zprod = sb("zprod", [P, H, ROWS, DH])
        v = sb("v", [P, H, ROWS, DH])
        rv = sb("rv", [P, H, ROWS, DH])
        rk = sb("rk", [P, H, ROWS + 1, DH])
        ru = sb("ru", [P, H, ROWS, DH])
        hs = sb("hs", [P, ROWS, H, DH])
        hsT = ru[:].rearrange("p h s d -> p (h s d)").rearrange("p (c n) -> p c n", c=2 * ROWS)
        wprod = prod[:, :, ROWS + 1:ROWS + 3, :].rearrange("p h s d -> p h (s d)").rearrange("p h (c j) -> p h c j", c=ROWS)
        rprod = hs[:].rearrange("p s h d -> p (s h d)").rearrange("p (h s d) -> p h s d", h=H, s=ROWS)
        dots = sb("dots", [P, H, ROWS, 2 * ROWS])
        rdots = sb("rdots", [P, H, ROWS, ROWS])
        be = sb("be", [P, ROWS, 2, H])
        br = sb("br", [P, ROWS, 2, H])
        ksum = sb("ksum", [P, H, 2 * ROWS])
        ik = sb("ik", [P, H, 2 * ROWS])
        mk = sb("mk", [P, H, 2 * ROWS])
        rkm = sb("rkm", [P, H, ROWS])
        rks = sb("rks", [P, H, ROWS])
        ub = sb("ub", [P, H, ROWS])
        rub = sb("rub", [P, H, ROWS])
        nrb = sb("nrb", [P, H, ROWS])
        eh = sb("eh", [P, H, DH])
        qd = sb("qd", [P, H, ROWS + 1])
        qr = sb("qr", [P, H])
        hmax = sb("hmax", [P, H])

        cen = sb("cen", [P, ROWS, D])
        sqr = sb("sqr", [P, ROWS, D])
        onorm = sb("onorm", [P, ROWS, D])
        oT = sb("oT", [P, ROWS // 2, P])
        st = sb("st", [P, 8, ROWS])
        hb = sb("hb", [P, ROWS, D])
        xf = sb("xf", [P, ROWS, D + 1])
        xfT = sb("xfT", [D, ROWS, P])
        lg = sb("lg", [P, 6, ROWS, E])
        gt = sb("gt", [P, 8, ROWS])
        g = sb("g", [P, ROWS, E])
        gT = sb("gT", [P, P])
        gx = [sb(f"gx{i}", [P, ROWS, D + 1]) for i in range(GX_RING)]
        gxT = [sb(f"gxT{i}", [D + 1, 512]) for i in range(2)]
        hT = [sb(f"hT{i}", [F, 512]) for i in range(2)]
        ysb = sb("ysb", [P, 512])
        yo = sb("yo", [P, ROWS, D])

        phase = ex[0:FEATS].rearrange("p h s d -> p (h s d)")[:, 0:T + 2 * P]
        phase_now = hs[0:FEATS].rearrange("p s h d -> p (s h d)")[:, 0:2 * P]
        flat_v = v[:].rearrange("p h s d -> p (h s d)")
        flat_rv = rv[:].rearrange("p h s d -> p (h s d)")
        flat_ru = ru[:].rearrange("p h s d -> p (h s d)")
        flat_kq = kq[:].rearrange("p h s d -> p (h s d)")
        flat_prod = prod[:].rearrange("p h s d -> p (h s d)")
        flat_u = u[:].rearrange("p h s d -> p (h s d)")
        dft = flat_prod[:, 0:TC * 2 * 3 * BINS].rearrange("p (c n) -> p c n", c=TC)
        wb = flat_kq[0:FEATS, 0:ROWS * HID]
        ge_enc = flat_kq[:, 1024:2048]
        hn_enc = flat_kq[:, 2048:4096]
        sq_enc = zprod[:].rearrange("p h s d -> p (h s d)")
        hid_ps = [l1_ps[0], l1_ps[1], ring_ps[0], ring_ps[1]]
        w1ext = flat_rv[0:FEATS, 0:HID]
        w2e = flat_rv[:, 128:192]
        b2e = flat_rv[:, 192:256]
        cs = flat_rv[0:FEATS, 256:264]
        fb = flat_rv[2 * BINS:3 * BINS, 264:265]
        gam_enc = flat_rv[:, 265:266]
        bet_enc = flat_rv[:, 266:267]
        wmean = flat_rv[0:FEATS, 267:268]
        re_im = flat_rv[0:3 * BINS, 272:288]
        tmp8 = [flat_rv[0:3 * BINS, 288 + 8 * i:296 + 8 * i] for i in range(5)]
        rs_enc = [flat_rv[:, 336 + 16 * i:352 + 16 * i] for i in range(3)]
        sig = flat_rv[:, 384:512].rearrange("p (b c) -> p b c", b=ROWS)
        ids = flat_rv[:, 512:512 + ROWS * TC].bitcast(I32).rearrange("p (b c) -> p b c", b=ROWS)
        slow_raw = flat_u[0:SLOW_CHUNK, 0:SLOW_CHUNKS * 2 * D].rearrange("p (c a d) -> p c a d", c=SLOW_CHUNKS, a=2)
        slowT_raw = flat_ru[:, 0:SLOW]
        outw_raw = flat_v[0:D, 0:HD]

        loaded = sem("loaded")
        b2_cleared = sem("b2_cleared")
        b2_loaded = sem("b2_loaded")
        setup_steps = sem("setup_steps")
        bins_summed = sem("bins_summed")
        bins_copied = sem("bins_copied")
        slow_turned = sem("slow_turned")
        slow_copied = sem("slow_copied")
        slow_sorted = sem("slow_sorted")
        outw_turned = sem("outw_turned")
        phase_copied = sem("phase_copied")
        hid_summed = sem("hid_summed")
        hid_squared = sem("hid_squared")
        hid_turned = sem("hid_turned")
        hid_gelu = sem("hid_gelu")
        token_summed = sem("token_summed")
        token_stored = sem("token_stored")
        v_did = {name: sem("v_" + name) for name in STEPS if name != "setup"}
        ring_full = sem("ring_full")
        ring_taken = sem("ring_taken")
        vec_full = sem("vec_full")
        rk_exp = sem("rk_exp")
        h_exp = sem("h_exp")
        gate_exp = sem("gate_exp")
        gx_ready = sem("gx_ready")
        l1_done = sem("l1_done")
        hT_ready = sem("hT_ready")
        l2_done = sem("l2_done")
        y_copied = sem("y_copied")
        z_summed = [sem(f"z_summed{i}") for i in range(2)]
        h_summed = [sem(f"h_summed{i}") for i in range(2)]
        hs_copied = [sem(f"hs_copied{i}") for i in range(2)]
        out_stored = sem("out_stored")

        block = ctx.enter_context(nc.Block())
        N_LOADS = 28

        def row(a):
            return a.rearrange("(a n) -> a n", a=1)

        def col(a):
            return a.rearrange("(n a) -> n a", a=1)

        def of_tile(t):
            return h_all[:, bass.ds(t, 1)].rearrange("p a b d -> p (a b) d")

        def done(eng, stage, tiles):
            for name in ("rec0", "rec1") if stage == "rec" else (stage,):
                wait(eng, v_did[name], tiles * STEPS[name])

        @block.sync
        def _(sp):
            n = [0]

            def load(dst, src):
                sp.dma_start(dst, src).then_inc(loaded, 16)
                n[0] += 1

            load(ids, x.rearrange("b (p c) -> p b c", c=TC))
            load(dft, dft_d)
            load(w1ext[0:BINS], tw1[BINS:2 * BINS, :])
            load(w1ext[BINS:2 * BINS], tw1[BINS:2 * BINS, :])
            load(w1ext[2 * BINS:3 * BINS], tw1[0:BINS, :])
            load(w1ext[3 * BINS:FEATS], row(tb1))
            load(fb, col(freq))
            load(phase, phase_d)
            load(ident[:], ident_d)
            load(gam_enc, col(tgam))
            load(bet_enc, col(tbet))
            load(w2e, tw2)
            load(b2e, row(tb2).broadcast_to([P, D]))
            load(slow_raw[:, :, 0, :], slow.rearrange("(c p) d -> p c d", p=SLOW_CHUNK))
            load(slow_raw[:, :, 1, :], slow.rearrange("(c p) d -> p c d", p=SLOW_CHUNK))
            load(outw_raw, outw)
            for half in (0, D):
                load(lngb[half:half + D, 0:1], col(lng))
                load(lngb[half:half + D, 1:2], col(lnb))
            load(rank[:], row(rank_d).broadcast_to([P, E]))
            load(gate_w[:], gw)
            load(gate_b[:], row(gb).broadcast_to([P, E]))
            load(w1[0:D], fw1.rearrange("e h f -> h e f"))
            load(w1[D:D + 1], fb1.unsqueeze(0))
            load(w2[:], fw2.rearrange("e f h -> f e h"))
            load(gamb[:, 0, :], row(fgam).broadcast_to([P, D]))
            load(gamb[:, 1, :], row(fbet).broadcast_to([P, D]))
            assert n[0] == N_LOADS, n
            sp.wait_ge(b2_cleared, 1)
            for r in range(ROWS):
                sp.dma_start(b2rows[r * E:(r + 1) * E, r, :], fb2).then_inc(b2_loaded, 16)

            with sp.Fori(0, NT) as t:
                sp.wait_ge(v_did["tail"], t * STEPS["tail"] + STEPS["tail"])
                sp.dma_start(out[:, bass.ds(t * P, P), :].rearrange("b p d -> p b d"), yo[:]).then_inc(out_stored, 16)
            sp.wait_ge(out_stored, 16 * NT)

        @block.gpsimd
        def _(pool):
            pool.memset(b2rows[:], 0.0).then_inc(b2_cleared, 1)

            def gate_inputs(t):
                done(pool, "gates", t + 1)
                for e in range(E):
                    if e >= GX_RING:
                        pool.wait_ge(ring_full, fill(t + 1, "gx", GROUPS * (e - GX_RING + 1) - 1) + 1)
                    elif not is_first(t):
                        pool.wait_ge(ring_full, fill(t, "gx", GROUPS * (E + e - GX_RING + 1) - 1) + 1)
                    pool.tensor_tensor(gx[e % GX_RING][:], xf[:],
                                       g[:, :, e:e + 1].broadcast_to([P, ROWS, D + 1]), ALU.mult).then_inc(gx_ready, 1)

            gate_inputs(0)
            with pool.Fori(1, NT - 2) as t:
                gate_inputs(t)
            gate_inputs(NT - 2)
            gate_inputs(NT - 1)

        @block.vector
        def _(dve):
            V = nc.vector

            def stage(name, t):
                return Stage(dve, v_did[name], name, t)

            def over_d(y, n=D):
                return y.unsqueeze(2).broadcast_to([P, ROWS, n])

            def run(steps):
                for _ in steps:
                    pass

            def weave(main, side, n):
                for _ in main:
                    for _ in range(n):
                        next(side, None)

            def norm(a, src):
                a.did(V.tensor_reduce(st[:, 0], src, AX, ALU.add))
                yield
                a.settle()
                a.did(V.tensor_scalar(st[:, 1], st[:, 0], 1.0 / D, None, ALU.mult))
                yield
                a.settle()
                a.did(V.tensor_tensor(cen[:], src, over_d(st[:, 1]), ALU.subtract))
                yield
                a.settle()
                a.did(V.tensor_tensor(sqr[:], cen[:], cen[:], ALU.mult))
                yield
                a.settle()
                a.did(V.tensor_reduce(st[:, 0], sqr[:], AX, ALU.add))
                yield
                a.settle()
                a.did(V.tensor_scalar(st[:, 2], st[:, 0], 1.0 / D, None, ALU.mult))
                yield
                a.settle()
                a.did(V.tensor_scalar(st[:, 1], st[:, 2], EPS, None, ALU.add))
                yield
                a.settle()
                yield from rsqrt(a, st[:, 3], st[:, 1], st[:, 0])

            def rsqrt(a, y, x, t):
                a.did(V.tensor_scalar(t.bitcast(I32), x.bitcast(I32), 1, None, ALU.logical_shift_right))
                yield
                a.settle()
                a.did(V.tensor_scalar(y.bitcast(I32), t.bitcast(I32), -1.0, RSQRT_SEED, ALU.mult, ALU.add))
                yield
                a.settle()
                for _ in range(NEWTON):
                    a.did(V.tensor_tensor(t, y, y, ALU.mult))
                    yield
                    a.settle()
                    a.did(V.scalar_tensor_tensor(out=t, in0=t, scalar=-0.5, in1=x, op0=ALU.mult, op1=ALU.mult))
                    yield
                    a.settle()
                    a.did(V.scalar_tensor_tensor(out=y, in0=t, scalar=1.5, in1=y, op0=ALU.add, op1=ALU.mult))
                    yield
                    a.settle()

            a = Stage(dve, setup_steps, "setup", 0)
            a.did(V.memset(rk[:, :, 0, :], 1.0))
            a.did(V.memset(dots[:], 0.0))
            a.did(V.memset(rdots[:], 0.0))
            a.did(V.memset(xf[:, :, D:D + 1], 1.0))
            dve.wait_ge(loaded, 16 * N_LOADS)
            a.then(V.tensor_scalar(sig, ids, 1.0 / 127.5, -1.0, ALU.mult, ALU.add))
            a.then(V.tensor_reduce(wmean, w1ext, AX, ALU.add))
            a.then(V.tensor_scalar(wmean, wmean, 1.0 / HID, None, ALU.mult))
            a.then(V.tensor_scalar(w1ext, w1ext, wmean, None, ALU.subtract))
            a.then(V.memset(cs, 1.0))
            dve.wait_ge(bins_summed, 1)
            a.then(V.tensor_copy(re_im, vec_ps[0:3 * BINS, 0:2 * ROWS]))
            re, im = re_im[:, 0:ROWS], re_im[:, ROWS:2 * ROWS]
            t0, t1, mag, zero, inv = tmp8
            a.then(V.tensor_tensor(t0, re, re, ALU.mult))
            a.then(V.tensor_tensor(t1, im, im, ALU.mult))
            a.then(V.tensor_tensor(t0, t0, t1, ALU.add))
            a.then(V.tensor_scalar(zero, t0, 0.0, None, ALU.is_equal))
            a.then(V.tensor_tensor(t1, t0, zero, ALU.add))
            run(rsqrt(a, inv, t1, mag))
            a.then(V.tensor_tensor(mag, t0, inv, ALU.mult))
            a.then(V.tensor_tensor(t0, re, inv, ALU.mult))
            a.then(V.tensor_tensor(cs[0:BINS], t0[0:BINS], zero[0:BINS], ALU.add))
            a.then(V.tensor_tensor(cs[BINS:2 * BINS], im[BINS:2 * BINS], inv[BINS:2 * BINS], ALU.mult))
            a.then(V.tensor_scalar(cs[2 * BINS:3 * BINS], mag[2 * BINS:3 * BINS], fb, None, ALU.mult))
            for b in range(ROWS):
                a.then(V.tensor_scalar(wb[:, b * HID:(b + 1) * HID], w1ext, cs[:, b:b + 1], None, ALU.mult))
            a.close()

            def encode(s):
                a = stage("encode", s)
                for k in range(PARTS):
                    dve.wait_ge(hid_squared, PARTS * s + (k + 1))
                    a.did(V.tensor_reduce(rs_enc[0][:, 4 * k:4 * k + 4],
                                          sq_enc[:, 512 * k:512 * k + 512].rearrange("p (b n) -> p b n", b=4), AX, ALU.add))
                a.settle()
                a.then(V.tensor_scalar(rs_enc[1], rs_enc[0], 1.0 / HID, EPS, ALU.mult, ALU.add))
                run(rsqrt(a, rs_enc[0], rs_enc[1], rs_enc[2]))
                wait(dve, hid_turned, PARTS * s)
                for k in range(PARTS):
                    r = rs_enc[0][:, 4 * k:4 * k + 4].unsqueeze(2).broadcast_to([P, 4, HID])
                    a.did(V.tensor_tensor(hn_enc[:, 512 * k:512 * k + 512].rearrange("p (b n) -> p b n", b=4),
                                          hid_ps[k][:].rearrange("p (b n) -> p b n", b=4), r, ALU.mult))
                a.close()

            def store_tokens(s):
                for k in range(2):
                    dve.wait_ge(token_summed, PARTS * s + (2 * k + 2))
                    V.tensor_tensor(of_tile(2 * s + k), token_ps[k][:].rearrange("p (b d) -> p b d", b=ROWS),
                                    b2e.unsqueeze(1).broadcast_to([P, ROWS, D]), ALU.add).then_inc(token_stored, 1)

            encode(0)
            with dve.Fori(1, PAIRS) as s:
                encode(s)
                store_tokens(s - 1)
            store_tokens(PAIRS - 1)
            dve.wait_ge(token_stored, NT)

            def front(t):
                a = stage("front", t)
                yield from norm(a, of_tile(t))
                a.did(V.tensor_tensor(sqr[:], cen[:], over_d(st[:, 3]), ALU.mult))
                a.did(V.tensor_tensor(st[:, 4], st[:, 2], st[:, 3], ALU.mult))
                yield
                a.settle()
                a.did(V.tensor_tensor(st[:, 4], st[:, 4], st[:, 3], ALU.mult))
                yield
                a.settle()
                a.did(V.tensor_scalar(st[:, 1], st[:, 4], EPS, None, ALU.add))
                yield
                a.settle()
                yield from rsqrt(a, st[:, 5], st[:, 1], st[:, 0])
                if not is_first(t):
                    dve.wait_ge(ring_full, fill(t - 2, "oT") + 1)
                a.did(V.tensor_tensor(onorm[:], sqr[:], over_d(st[:, 5]), ALU.mult))
                a.did(V.tensor_tensor(of_tile(t), of_tile(t), sqr[:], ALU.add))
                a.close()

            def mix(t):
                a = stage("mix", t)
                dve.wait_ge(ring_taken, fill(t - 1, "kq", ROWS - 1) + 1)
                a.did(V.scalar_tensor_tensor(out=kq[:], in0=ex[:], scalar=1.0, in1=kq[:], op0=ALU.min, op1=ALU.add))
                yield
                dve.wait_ge(ring_taken, fill(t - 1, "v", ROWS - 1) + 1)
                a.did(V.tensor_scalar(be[:], be[:], 1.0, None, ALU.add))
                a.settle()
                a.settle()
                a.did(V.reciprocal(br[:], be[:]))
                a.did(V.tensor_reduce(ksum[:], kq[:], AX, ALU.add))
                yield
                a.settle()
                a.did(V.reciprocal(ik[:], ksum[:]))
                yield
                a.settle()
                beta = br[:, :, 0, :].rearrange("p s h -> p h s")
                a.did(V.tensor_copy(mk[:, :, 1::2], ik[:, :, 1::2]))
                a.did(V.tensor_tensor(ub[:], ik[:, :, 0::2], beta, ALU.mult))
                yield
                a.settle()
                a.did(V.scalar_tensor_tensor(out=mk[:, :, 0::2], in0=ub[:], scalar=-1.0, in1=ik[:, :, 0::2],
                                             op0=ALU.mult, op1=ALU.mult))
                yield
                a.close()

            def dot(t):
                a = stage("dots", t)
                for half in range(2):
                    wait(dve, h_summed[half], t * ROWS)
                for i in range(ROWS):
                    m = 2 * ROWS - 1 - 2 * i
                    buf = prod if i % 2 == 0 else ex
                    a.did(V.tensor_tensor(buf[:, :, 0:m, :], kq[:, :, 2 * i + 1:, :],
                                          kq[:, :, 2 * i:2 * i + 1, :].broadcast_to([P, H, m, DH]), ALU.mult))
                    yield
                    a.settle()
                    a.did(V.tensor_reduce(dots[:, :, i, 2 * i + 1:], buf[:, :, 0:m, :], AX, ALU.add))
                    yield
                a.settle()
                a.did(V.tensor_tensor(dots[:], dots[:], mk[:].unsqueeze(2).broadcast_to([P, H, ROWS, 2 * ROWS]), ALU.mult))
                yield
                a.close()

            def init(t):
                a = stage("init", t)
                dve.wait_ge(ring_taken, fill(t - 1, "rv", ROWS // 2 - 1) + 1)
                a.did(V.tensor_tensor(u[:], v[:], ub[:].unsqueeze(3).broadcast_to([P, H, ROWS, DH]), ALU.mult))
                yield
                a.did(V.tensor_tensor(ru[:], rv[:], rub[:].unsqueeze(3).broadcast_to([P, H, ROWS, DH]), ALU.mult))
                yield
                a.close()

            def rk_prep(t):
                a = stage("rkprep", t)
                dve.wait_ge(ring_taken, fill(t, "rk", ROWS // 2 - 1) + 1)
                a.did(V.tensor_reduce(rkm[:], rk[:, :, 1:, :], AX, ALU.max))
                yield
                a.settle()
                a.did(V.tensor_tensor(rk[:, :, 1:, :], rk[:, :, 1:, :],
                                      rkm[:].unsqueeze(3).broadcast_to([P, H, ROWS, DH]), ALU.subtract))
                a.close()

            def rk_sum(t):
                a = stage("rksum", t)
                dve.wait_ge(rk_exp, t + 1)
                a.did(V.tensor_reduce(rkm[:], rk[:, :, 1:, :], AX, ALU.add))
                yield
                a.settle()
                a.did(V.reciprocal(rks[:], rkm[:]))
                yield
                a.settle()
                a.did(V.tensor_tensor(rub[:], rks[:], br[:, :, 1, :].rearrange("p s h -> p h s"), ALU.mult))
                yield
                a.settle()
                a.did(V.scalar_tensor_tensor(out=nrb[:], in0=rub[:], scalar=-1.0, in1=rks[:], op0=ALU.mult, op1=ALU.mult))
                yield
                a.close()

            def r_dot(t):
                a = stage("rdots", t)
                if not is_first(t):
                    dve.wait_ge(ring_full, fill(t, "hsT", ROWS // 2 - 1) + 1)
                for i in range(ROWS - 1):
                    m = ROWS - 1 - i
                    a.did(V.tensor_tensor(rprod[:, :, 0:m, :], rk[:, :, i + 2:, :],
                                           rk[:, :, i + 1:i + 2, :].broadcast_to([P, H, m, DH]), ALU.mult))
                    yield
                    a.settle()
                    a.did(V.tensor_reduce(rdots[:, :, i, i + 1:], rprod[:, :, 0:m, :], AX, ALU.add))
                    yield
                    a.settle()
                a.did(V.tensor_tensor(rdots[:], rdots[:], nrb[:].unsqueeze(2).broadcast_to([P, H, ROWS, ROWS]), ALU.mult))
                yield
                a.settle()
                a.close()

            def delta(t):
                a = stage("delta", t)
                for l in range(ROWS - 1, 0, -1):
                    m = ROWS - l
                    a.did(V.tensor_tensor(prod[:, :, 0:l, 0:m],
                                          dots[:, :, 0:l, 2 * l:2 * l + 1].broadcast_to([P, H, l, m]),
                                          dots[:, :, l:l + 1, 2 * l + 1::2].broadcast_to([P, H, l, m]), ALU.mult))
                    yield
                    a.settle()
                    a.did(V.tensor_tensor(dots[:, :, 0:l, 2 * l + 1::2], dots[:, :, 0:l, 2 * l + 1::2],
                                          prod[:, :, 0:l, 0:m], ALU.add))
                    yield
                    a.settle()
                a.close()

            def r_delta(t):
                a = stage("rdelta", t)
                a.did(V.memset(rdots[:].rearrange("p h i j -> p h (i j)")[:, :, 0::ROWS + 1], 1.0))
                for j in range(1, ROWS - 1):
                    m = ROWS - 1 - j
                    a.did(V.tensor_tensor(rprod[:, :, 0:j, 0:m],
                                          rdots[:, :, 0:j, j:j + 1].broadcast_to([P, H, j, m]),
                                          rdots[:, :, j:j + 1, j + 1:].broadcast_to([P, H, j, m]), ALU.mult))
                    yield
                    a.settle()
                    a.did(V.tensor_tensor(rdots[:, :, 0:j, j + 1:], rdots[:, :, 0:j, j + 1:], rprod[:, :, 0:j, 0:m],
                                          ALU.add))
                    yield
                    a.settle()
                a.close()

            def rec(t, half):
                a = stage(f"rec{half}", t)
                hh = slice(half * HH, (half + 1) * HH)
                p_, qd_, qr_, eh_, hmax_ = prod[:, hh], qd[:, hh], qr[:, hh], eh[:, hh], hmax[:, hh]
                w_ = wprod[:, hh]
                h_sum = h_ps[half][:, 0:HH * DH].rearrange("p (h d) -> p h d", h=HH)

                def z_products(i):
                    m = i + 1
                    wait(dve, z_summed[half], t * ROWS + i)
                    a.did(V.tensor_tensor(zprod[:, hh, 0:m, :],
                                          dots[:, hh, 0:m, 2 * i + 1].unsqueeze(3).broadcast_to([P, HH, m, DH]),
                                          u[:, hh, 0:m, :], ALU.mult))
                    assert a.n == REC_Z(i)

                z_products(0)
                yield
                for i in range(ROWS):
                    m = i + 1
                    if i == 0:
                        a.did(V.tensor_reduce(qd_[:, :, 1:2], rk[:, hh, 1:2, :], AX, ALU.add))
                        yield
                        a.settle()
                        a.did(V.tensor_scalar(qd_[:, :, 1:2], qd_[:, :, 1:2], 1.0 / DH, None, ALU.mult))
                        yield
                        a.settle()
                    else:
                        dve.wait_ge(h_exp, t * H_EXPS + (2 * (i - 1) + half + 1))
                        a.did(V.tensor_tensor(p_[:, :, 0:m + 1, :], rk[:, hh, 0:m + 1, :],
                                              eh_.unsqueeze(2).broadcast_to([P, HH, m + 1, DH]), ALU.mult))
                        yield
                        a.settle()
                        a.did(V.tensor_reduce(qd_[:, :, 0:m + 1], p_[:, :, 0:m + 1, :], AX, ALU.add))
                        yield
                        a.settle()
                        a.did(V.tensor_tensor(w_[:, :, 0:m, 0:m], rdots[:, hh, 0:m, 0:m],
                                              qd_[:, :, 1:m + 1].unsqueeze(2).broadcast_to([P, HH, m, m]), ALU.mult))
                        a.did(V.reciprocal(qr_, qd_[:, :, 0]))
                        yield
                        a.settle()
                        a.did(V.tensor_reduce(qd_[:, :, 1:m + 1], w_[:, :, 0:m, 0:m], AX, ALU.add))
                        yield
                        a.settle()
                        a.did(V.tensor_tensor(qd_[:, :, 1:m + 1], qd_[:, :, 1:m + 1],
                                              qr_.unsqueeze(2).broadcast_to([P, HH, m]), ALU.mult))
                        yield
                        a.settle()
                    a.did(V.tensor_tensor(p_[:, :, 0:m, :], ru[:, hh, 0:m, :],
                                          qd_[:, :, 1:m + 1].unsqueeze(3).broadcast_to([P, HH, m, DH]), ALU.mult))
                    assert a.n == REC_P2(i)
                    yield
                    if i < ROWS - 1:
                        z_products(i + 1)
                        yield
                        dve.wait_ge(h_summed[half], t * ROWS + (i + 1))
                        a.did(V.tensor_reduce(hmax_, h_sum, AX, ALU.max))
                        yield
                        a.settle()
                        a.did(V.tensor_tensor(eh_, h_sum, hmax_.unsqueeze(2).broadcast_to([P, HH, DH]), ALU.subtract))
                        assert a.n == REC_EXP(i)
                        yield
                a.close()

            def back(t):
                a = stage("back", t)
                dve.wait_ge(vec_full, t * 3 + 1)
                a.did(V.tensor_tensor(hb[:], of_tile(t), vec_ps[:].rearrange("p (b d) -> p b d", b=ROWS), ALU.add))
                yield
                a.settle()
                yield from norm(a, hb[:])
                wait(dve, gx_ready, t * E)
                a.did(V.tensor_tensor(xf[:, :, 0:D], cen[:], over_d(st[:, 3]), ALU.mult))
                a.close()

            def gates(t):
                a = stage("gates", t)
                rk_bc = rank[:].unsqueeze(1).broadcast_to([P, ROWS, E])
                dve.wait_ge(vec_full, t * 3 + 2)
                a.did(V.tensor_tensor(lg[:, 0], vec_ps[:, 0:ROWS * E].rearrange("p (b e) -> p b e", b=ROWS),
                                       gate_b[:].unsqueeze(1).broadcast_to([P, ROWS, E]), ALU.add))
                yield
                a.settle()
                for k, (src, m, one) in enumerate(((0, 0, 2), (1, 2, 4))):
                    a.did(V.tensor_reduce(gt[:, m], lg[:, src], AX, ALU.max))
                    yield
                    a.settle()
                    a.did(V.tensor_tensor(lg[:, 5], lg[:, src], over_d(gt[:, m], E), ALU.is_equal))
                    yield
                    a.settle()
                    a.did(V.tensor_tensor(lg[:, 5], lg[:, 5], rk_bc, ALU.mult))
                    yield
                    a.settle()
                    a.did(V.tensor_reduce(gt[:, m + 1], lg[:, 5], AX, ALU.max))
                    yield
                    a.settle()
                    a.did(V.tensor_tensor(lg[:, one], lg[:, 5], over_d(gt[:, m + 1], E), ALU.is_equal))
                    yield
                    a.settle()
                    if k == 0:
                        a.did(V.scalar_tensor_tensor(out=lg[:, 1], in0=lg[:, 2], scalar=-BIG, in1=lg[:, 0],
                                                      op0=ALU.mult, op1=ALU.add))
                        yield
                        a.settle()
                a.did(V.tensor_tensor(gt[:, 4], gt[:, 2], gt[:, 0], ALU.subtract))
                assert a.n == GATE_EXP

                dve.wait_ge(gate_exp, t + 1)
                a.did(V.tensor_scalar(gt[:, 6], gt[:, 5], 1.0, None, ALU.add))
                yield
                a.settle()
                a.did(V.reciprocal(gt[:, 6], gt[:, 6]))
                yield
                a.settle()
                a.did(V.tensor_tensor(lg[:, 3], lg[:, 2], over_d(gt[:, 6], E), ALU.mult))
                a.did(V.tensor_tensor(gt[:, 7], gt[:, 6], gt[:, 5], ALU.mult))
                yield
                a.settle()
                a.did(V.tensor_tensor(lg[:, 5], lg[:, 4], over_d(gt[:, 7], E), ALU.mult))
                yield
                a.settle()
                if not is_first(t):
                    dve.wait_ge(ring_full, fill(t, "gT") + 1)
                a.did(V.tensor_tensor(g[:], lg[:, 3], lg[:, 5], ALU.add))
                a.close()

            def tail(t):
                a = stage("tail", t)
                dve.wait_ge(vec_full, t * 3 + 3)
                a.did(V.tensor_tensor(cen[:], vec_ps[:].rearrange("p (b d) -> p b d", b=ROWS), xf[:, :, 0:D], ALU.add))
                yield
                a.settle()
                yield from norm(a, cen[:])
                a.did(V.tensor_tensor(sqr[:], cen[:], over_d(st[:, 3]), ALU.mult))
                yield
                a.settle()
                a.did(V.tensor_tensor(sqr[:], sqr[:], gamb[:, 0, :].unsqueeze(1).broadcast_to([P, ROWS, D]), ALU.mult))
                yield
                a.settle()
                a.did(V.tensor_tensor(sqr[:], sqr[:], gamb[:, 1, :].unsqueeze(1).broadcast_to([P, ROWS, D]), ALU.add))
                yield
                a.settle()
                wait(dve, out_stored, t * 16)
                a.did(V.tensor_tensor(yo[:], sqr[:], hb[:], ALU.add))
                a.close()

            def iteration(t):
                first = is_first(t)
                ahead = not isinstance(t, int) or t < NT - 2
                mixing = mix(t)
                dotting, small = dot(t), chain(rk_sum(t), init(t), r_dot(t), r_delta(t))
                if first:
                    run(mixing)
                    run(rk_prep(t))
                    next(dotting)
                else:
                    before = back(t - 1)
                    run(islice(mixing, MIX_BEFORE_BACK))
                    weave(mixing, before, BACK_PER_MIX)
                    run(before)
                    run(rk_prep(t))
                    gating = gates(t - 1)
                    weave(islice(dotting, 2), gating, GATES_PER_DOT)
                    run(gating)
                weave(dotting, small, SMALL_PER_DOT)
                weave(delta(t), small, 1)
                run(small)
                halves = rec(t, 0), rec(t, 1)
                before, after = iter(() if first else tail(t - 1)), iter(front(t + 2) if ahead else ())
                for k, _ in enumerate(halves[0]):
                    next(halves[1], None)
                    if k < TAIL_FROM:
                        next(after, None)
                    else:
                        next(before, None)
                run(halves[1])
                run(after)
                run(before)

            run(front(0))
            run(front(1))
            iteration(0)
            iteration(1)
            with dve.Fori(2, NT - 2) as t:
                iteration(t)
            iteration(NT - 2)
            iteration(NT - 1)
            run(back(NT - 1))
            run(gates(NT - 1))
            run(tail(NT - 1))

        @block.tensor
        def _(pe):
            T_ = nc.tensor
            pe.wait_ge(loaded, 16 * N_LOADS)
            pe.wait_ge(setup_steps, 5)
            for part in range(2):
                for c in range(TC):
                    mm = T_.matmul(vec_ps[0:3 * BINS, part * ROWS:(part + 1) * ROWS],
                                   dft[:, c, part * 3 * BINS:(part + 1) * 3 * BINS], sig[:, :, c],
                                   start=(c == 0), stop=(c == TC - 1))
            mm.then_inc(bins_summed, 1)
            for c in range(SLOW_CHUNKS):
                wait(pe, slow_copied, c - 1)
                T_.transpose(ring_ps[c % 2][:, 0:SLOW_CHUNK], slow_raw[:, c].rearrange("p a d -> p (a d)"),
                             ident[0:SLOW_CHUNK, 0:SLOW_CHUNK]).then_inc(slow_turned, 1)
            pe.wait_ge(slow_copied, SLOW_CHUNKS)
            for c in range(2):
                mm = T_.transpose(ring_ps[0][:, c * D:(c + 1) * D], outw_raw[:, c * P:(c + 1) * P], ident[0:D, 0:D])
            mm.then_inc(outw_turned, 1)

            def hidden(s):
                pe.wait_ge(phase_copied, s + 1)
                for k in range(PARTS):
                    T_.matmul(hid_ps[k][:], phase_now[:, (k // 2) * P:(k // 2 + 1) * P],
                              wb[:, 512 * (k % 2):512 * (k % 2) + 512], start=True, stop=True).then_inc(hid_summed, 1)

            def turn(s, k):
                wait(pe, hid_gelu, PARTS * s + (k - 1))
                for b in range(4):
                    mm = T_.transpose(h_ps[k % 2][:, b * P:(b + 1) * P], hn_enc[:, 512 * k + b * P:512 * k + (b + 1) * P],
                                      ident[:])
                mm.then_inc(hid_turned, 1)

            def tokens(s, k):
                pe.wait_ge(hid_gelu, PARTS * s + (k + 1))
                if k % 2 == 0:
                    wait(pe, token_stored, 2 * s + (k // 2 - 1))
                for b in range(4):
                    r = 4 * (k % 2) + b
                    mm = T_.matmul(token_ps[k // 2][:, r * D:(r + 1) * D],
                                   ge_enc[:, 512 * (k % 2) + b * P:512 * (k % 2) + (b + 1) * P], w2e, start=True, stop=True)
                mm.then_inc(token_summed, 1)

            def encode(s):
                pe.wait_ge(v_did["encode"], s * STEPS["encode"] + STEPS["encode"])
                if not (isinstance(s, int) and s == PAIRS - 1):
                    hidden(s + 1)
                turn(s, 0)
                for k in range(PARTS):
                    if k < PARTS - 1:
                        turn(s, k + 1)
                    tokens(s, k)

            pe.wait_ge(setup_steps, STEPS["setup"])
            hidden(0)
            encode(0)
            with pe.Fori(1, PAIRS - 1) as s:
                encode(s)
            encode(PAIRS - 1)

            def event(t, what, i, write):
                wait(pe, ring_taken, fill(t, what, i) - 1)
                write(ring_ps[parity(t, what, i)]).then_inc(ring_full, 1)

            def project(ps, at, r, c0, n):
                half = (r % 2) * D
                return T_.matmul(ps[:, at:at + n], oT[half:half + D, r // 2, :], slowT[half:half + D, c0:c0 + n],
                                 start=True, stop=True)

            def o_turned(t):
                done(pe, "front", t + 1)

                def write(ps):
                    for c in range(ROWS // 2):
                        mm = T_.transpose(ps[:, c * P:(c + 1) * P],
                                          onorm[:, 2 * c:2 * c + 2, :].rearrange("p b d -> p (b d)"), ident[:])
                    return mm
                event(t - 1, "oT", 0, write)
                pe.wait_ge(ring_taken, fill(t - 1, "oT") + 1)

            def ahead(t, what, i):
                if what == "kq":
                    event(t - 1, "kq", i, lambda ps: project(ps, 0, i, KQC, 2 * HD))
                elif what == "v":
                    event(t - 1, "v", i, lambda ps: project(ps, 0, i, VC, HD + 2 * H))
                else:
                    pair(t - 1, "rv", i, RVC)

            def pair(t, what, i, c0):
                r = 4 * (i // 2) + i % 2

                def write(ps):
                    project(ps, 0, r, c0, HD)
                    return project(ps, HD, r + 2, c0, HD)
                event(t, what, i, write)

            def h_turned(t):
                for i in range(ROWS // 2):
                    for half in range(2):
                        pe.wait_ge(hs_copied[half], t * ROWS + (2 * i + 2))

                    def write(ps):
                        for k in range(4):
                            r, c = 2 * i + k // 2, k % 2
                            mm = T_.transpose(ps[:, k * P:(k + 1) * P],
                                              hs[:, r, 4 * c:4 * c + 4, :].rearrange("p h d -> p (h d)"), ident[:])
                        return mm
                    event(t + 1, "hsT", i, write)
                pe.wait_ge(ring_taken, fill(t + 1, "hsT", ROWS // 2 - 1) + 1)
                if is_first(t):
                    pe.wait_ge(token_stored, NT)
                else:
                    pe.wait_ge(v_did["tail"], (t - 1) * STEPS["tail"] + 1)
                for r in range(ROWS):
                    for c in range(2):
                        mm = T_.matmul(vec_ps[:, r * D:(r + 1) * D], hsT[:, 2 * r + c, :], outT[:, c, :],
                                       start=(c == 0), stop=(c == 1))
                mm.then_inc(vec_full, 1)

            def gate_logits(t):
                done(pe, "back", t + 1)
                for i in range(2):
                    def write(ps):
                        for k in range(4):
                            mm = T_.transpose(ps[0:D + 1, k * P:(k + 1) * P], xf[:, 4 * i + k, :], ident[:])
                        return mm
                    event(t + 1, "xfT", i, write)
                pe.wait_ge(ring_taken, fill(t + 1, "xfT", 1) + 1)
                for r in range(ROWS):
                    mm = T_.matmul(vec_ps[:, r * E:(r + 1) * E], xfT[:, r, :], gate_w[:], start=True, stop=True)
                mm.then_inc(vec_full, 1)
                done(pe, "gates", t + 1)
                event(t + 1, "gT", 0, lambda ps: T_.transpose(ps[:, 0:P], g[:].rearrange("p b e -> p (b e)"), ident[:]))

            def recurrence(t, last):
                def summed(half, src, m, last):
                    for j in range(m):
                        mm = T_.matmul(h_ps[half][:, 0:HH * DH], ident[:], src[:, half * HH:(half + 1) * HH, j, :],
                                       start=(j == 0 and not last), stop=(j == m - 1 and last), skip_group_check=True)
                    return mm

                for i in range(ROWS):
                    for half in range(2):
                        pe.wait_ge(v_did[f"rec{half}"], t * STEPS[f"rec{half}"] + REC_Z(i))
                        wait(pe, hs_copied[half], t * ROWS + i)
                        summed(half, zprod, i + 1, False).then_inc(z_summed[half], 1)
                    for half in range(2):
                        pe.wait_ge(v_did[f"rec{half}"], t * STEPS[f"rec{half}"] + REC_P2(i))
                        summed(half, prod, i + 1, True).then_inc(h_summed[half], 1)
                    if not last:
                        for one in BESIDE[i]:
                            ahead(t + 1, *one)
                    if not is_first(t):
                        experts(t - 1, *slots_beside(i))
                        if i == Y_ROW:
                            y_turned(t - 1)

            def experts(t, lo=0, hi=FFN_SLOTS):
                base = t * FFN_STEPS
                for slot in range(lo, hi):
                    if slot < FFN_STEPS:
                        e, grp = slot // GROUPS, slot % GROUPS
                        pe.wait_ge(gx_ready, t * E + (e + 1))

                        def write(ps):
                            for k in range(GROWS):
                                mm = T_.transpose(ps[0:D + 1, k * P:(k + 1) * P],
                                                  gx[e % GX_RING][:, GROWS * grp + k, :], ident[:])
                            return mm
                        event(t + 1, "gx", slot, write)
                    k = slot - 1
                    if 0 <= k < FFN_STEPS:
                        pe.wait_ge(ring_taken, fill(t + 1, "gx", k) + 1)
                        if k >= 2:
                            pe.wait_ge(hT_ready, base + (k - 1))
                        T_.matmul(l1_ps[k % 2][:], w1[:, k // GROUPS, :], gxT[k % 2][:], start=True,
                                  stop=True).then_inc(l1_done, 1)
                    k = slot - 2
                    if 0 <= k < FFN_STEPS:
                        e, grp = k // GROUPS, k % GROUPS
                        part = slice(grp * D, (grp + 1) * D)
                        pe.wait_ge(hT_ready, base + (k + 1))
                        if e == 0:
                            wait(pe, y_copied, t)
                        T_.matmul(y_ps[part, :], w2[:, e, :], hT[k % 2][:], start=(e == 0), stop=(e == E - 1),
                                  skip_group_check=True).then_inc(l2_done, 1)
                        if e == 1:
                            if grp == 0:
                                if is_first(t):
                                    pe.wait_ge(b2_loaded, 16 * ROWS)
                                pe.wait_ge(ring_taken, fill(t + 1, "gT") + 1)
                            for q in range(GROWS):
                                T_.matmul(y_ps[part, q * P:(q + 1) * P], b2rows[:, GROWS * grp + q, :], gT[:],
                                          start=False, stop=False, skip_group_check=True)

            def y_turned(t):
                pe.wait_ge(y_copied, t + 1)
                pe.wait_ge(v_did["gates"], t * STEPS["gates"] + 1)
                for q in range(GROWS):
                    mm = T_.transpose(vec_ps[:].rearrange("p (a q d) -> p q a d", a=GROUPS, q=GROWS)[:, q],
                                      ysb[:, q * P:(q + 1) * P], ident[:])
                mm.then_inc(vec_full, 1)

            def iteration(t):
                first, last = is_first(t), isinstance(t, int) and t == NT - 1
                if not first:
                    h_turned(t - 1)
                for i in range(ROWS // 2):
                    pair(t, "rk", i, RKC)
                if not first:
                    gate_logits(t - 1)
                    experts(t - 1, 0, FFN_BEFORE)
                if not last:
                    o_turned(t + 1)
                recurrence(t, last)

            pe.wait_ge(slow_sorted, SORTS)
            o_turned(0)
            for one in sum(BESIDE, []):
                ahead(0, *one)
            iteration(0)
            iteration(1)
            with pe.Fori(2, NT - 1) as t:
                iteration(t)
            iteration(NT - 1)
            h_turned(NT - 1)
            gate_logits(NT - 1)
            experts(NT - 1)
            y_turned(NT - 1)

        @block.scalar
        def _(act):
            S = nc.scalar
            act.wait_ge(loaded, 16 * N_LOADS)
            for c in range(SLOW_CHUNKS):
                act.wait_ge(slow_turned, c + 1)
                S.copy(slowT_raw[:, c * SLOW_CHUNK:(c + 1) * SLOW_CHUNK], ring_ps[c % 2][:, 0:SLOW_CHUNK]).then_inc(slow_copied, 1)
            act.wait_ge(slow_copied, SLOW_CHUNKS)
            raw = slowT_raw.rearrange("p (h m) -> p h m", h=H)
            kqcols = slowT[:, KQC:KQC + 2 * HD].rearrange("p (h j d) -> p h j d", h=H, j=2)
            sorts = [(kqcols[:, :, 0, :], raw[:, :, DH:2 * DH]), (kqcols[:, :, 1, :], raw[:, :, 0:DH])]
            for c0, m0 in ((VC, 2 * DH), (RVC, 4 * DH), (RKC, 3 * DH)):
                sorts.append((slowT[:, c0:c0 + HD].rearrange("p (h d) -> p h d", h=H), raw[:, :, m0:m0 + DH]))
            for i in range(2):
                sorts.append((slowT[:, VC + HD + i * H:VC + HD + (i + 1) * H], raw[:, :, 5 * DH + i]))
            for dst, src in sorts:
                S.copy(dst, src).then_inc(slow_sorted, 1)
            act.wait_ge(outw_turned, 1)
            S.copy(outT[:].rearrange("p c d -> p (c d)"), ring_ps[0][:, 0:2 * D]).then_inc(slow_sorted, 1)
            assert len(sorts) + 1 == SORTS

            def copy_phases(s):
                S.copy(phase_now, phase[:, bass.ds(s * 2 * P, 2 * P)]).then_inc(phase_copied, 1)

            def squares(s):
                for k in range(PARTS):
                    act.wait_ge(hid_summed, PARTS * s + (k + 1))
                    S.activation(sq_enc[:, 512 * k:512 * k + 512], hid_ps[k][:], ACT.Square).then_inc(hid_squared, 1)
                copy_phases(s + 1)

            def encode(s):
                if not (isinstance(s, int) and s == PAIRS - 1):
                    squares(s + 1)
                for k in range(PARTS):
                    act.wait_ge(hid_turned, PARTS * s + (k + 1))
                    wait(act, token_summed, PARTS * s + (k - 1))
                    S.activation(ge_enc[:, 512 * (k % 2):512 * (k % 2) + 512], h_ps[k % 2][:], ACT.Gelu, bias=bet_enc,
                                 scale=gam_enc).then_inc(hid_gelu, 1)

            copy_phases(0)
            squares(0)
            encode(0)
            with act.Fori(1, PAIRS - 1) as s:
                encode(s)
            encode(PAIRS - 1)
            act.wait_ge(phase_copied, PAIRS + 1)
            act.wait_ge(token_stored, NT)

            def take(t, what, i, copies):
                act.wait_ge(ring_full, fill(t, what, i) + 1)
                q = None
                for f in copies(ring_ps[parity(t, what, i)]):
                    q = f()
                q.then_inc(ring_taken, 1)

            def o_taken(t):
                take(t - 1, "oT", 0, lambda ps: [lambda: S.activation(
                    oT[:].rearrange("p c n -> p (c n)"), ps[:], ACT.Identity, bias=lngb[:, 1:2], scale=lngb[:, 0:1])])

            def ahead_taken(t, what, r):
                def kq_copies(ps):
                    src = ps[:].rearrange("p (h j d) -> p h j d", h=H, j=2)
                    return [lambda: S.activation(ex[:, :, 2 * r:2 * r + 2, :], src, ACT.Exp),
                            lambda: S.activation(kq[:, :, 2 * r:2 * r + 2, :], src, ACT.Relu)]

                def v_copies(ps):
                    return [lambda: S.activation(be[:, r].rearrange("p a h -> p (a h)"), ps[:, HD:HD + 2 * H],
                                                 ACT.Exp, scale=-1.0),
                            lambda: S.copy(v[:, :, r, :], ps[:, 0:HD].rearrange("p (h d) -> p h d", h=H))]
                if what == "rv":
                    pair_taken(t - 1, "rv", r, rv, 0)
                else:
                    take(t - 1, what, r, kq_copies if what == "kq" else v_copies)

            def pair_taken(t, what, i, dst, slot0):
                lo = slot0 + 4 * (i // 2) + i % 2
                take(t, what, i, lambda ps: [lambda: S.copy(
                    dst[:, :, lo:lo + 3:2, :].rearrange("p h s d -> p s h d"),
                    ps[:].rearrange("p (s h d) -> p s h d", s=2, h=H))])

            def rk_taken(t):
                done(act, "rec", t)
                for i in range(ROWS // 2):
                    pair_taken(t, "rk", i, rk, 1)

            def rk_exps(t):
                act.wait_ge(v_did["rkprep"], t * STEPS["rkprep"] + STEPS["rkprep"])
                S.activation(rk[:, :, 1:, :], rk[:, :, 1:, :], ACT.Exp).then_inc(rk_exp, 1)

            def h_taken(t):
                for i in range(ROWS // 2):
                    take(t + 1, "hsT", i, lambda ps: [lambda: S.copy(
                        hsT[:, 4 * i:4 * i + 4, :].rearrange("p c n -> p (c n)"), ps[:])])

            def xf_taken(t):
                for i in range(2):
                    take(t + 1, "xfT", i, lambda ps: [lambda: S.copy(
                        xfT[:, 4 * i:4 * i + 4, :].rearrange("p c n -> p (c n)"), ps[0:D, :])])

            def gates_taken(t):
                act.wait_ge(v_did["gates"], t * STEPS["gates"] + GATE_EXP)
                S.activation(gt[:, 5], gt[:, 4], ACT.Exp).then_inc(gate_exp, 1)
                take(t + 1, "gT", 0, lambda ps: [lambda: S.copy(gT[:], ps[:, 0:P])])

            def experts(t, lo=0, hi=FFN_SLOTS):
                base = t * FFN_STEPS
                for slot in range(lo, hi):
                    if slot < FFN_STEPS:
                        if slot >= 2:
                            act.wait_ge(l1_done, base + (slot - 1))
                        take(t + 1, "gx", slot, lambda ps: [lambda: S.copy(gxT[slot % 2][:], ps[0:D + 1, :])])
                    k = slot - 1
                    if 0 <= k < FFN_STEPS:
                        act.wait_ge(l1_done, base + (k + 1))
                        if k >= 2:
                            act.wait_ge(l2_done, base + (k - 1))
                        S.activation(hT[k % 2][:], l1_ps[k % 2][:], ACT.Relu).then_inc(hT_ready, 1)

            def y_taken(t):
                act.wait_ge(l2_done, t * FFN_STEPS + FFN_STEPS)
                S.copy(ysb[:], y_ps[:]).then_inc(y_copied, 1)

            def iteration(t):
                last = isinstance(t, int) and t == NT - 1
                first = is_first(t)
                if not first:
                    h_taken(t - 1)
                rk_taken(t)
                if not first:
                    xf_taken(t - 1)
                rk_exps(t)
                if not first:
                    gates_taken(t - 1)
                if not first:
                    experts(t - 1, 0, FFN_BEFORE)
                if not last:
                    o_taken(t + 1)
                    done(act, "dots", t + 1)
                    done(act, "init", t + 1)
                for i in range(ROWS):
                    for half in range(2):
                        if i < ROWS - 1:
                            act.wait_ge(v_did[f"rec{half}"], t * STEPS[f"rec{half}"] + REC_EXP(i))
                            part = eh[:, half * HH:(half + 1) * HH]
                            S.activation(part, part, ACT.Exp).then_inc(h_exp, 1)
                        else:
                            act.wait_ge(h_summed[half], t * ROWS + ROWS)
                        S.copy(hs[:, i, half * HH:(half + 1) * HH],
                               h_ps[half][:, 0:HH * DH].rearrange("p (h d) -> p h d", h=HH)).then_inc(hs_copied[half], 1)
                    if not last:
                        for one in BESIDE[i]:
                            ahead_taken(t + 1, *one)
                    if not first:
                        experts(t - 1, *slots_beside(i))
                        if i == Y_ROW:
                            y_taken(t - 1)

            act.wait_ge(slow_sorted, SORTS)
            o_taken(0)
            for one in sum(BESIDE, []):
                ahead_taken(0, *one)
            iteration(0)
            iteration(1)
            with act.Fori(2, NT - 1) as t:
                iteration(t)
            iteration(NT - 1)
            h_taken(NT - 1)
            xf_taken(NT - 1)
            gates_taken(NT - 1)
            experts(NT - 1)
            y_taken(NT - 1)


_INS = ["x", "L0_tok_freq_bands", "L0_tok_w1", "L0_tok_b1", "L0_tok_gamma", "L0_tok_beta", "L0_tok_w2", "L0_tok_b2",
        "L0_attn_slow_W", "L0_attn_out_W", "L0_attn_ln_g", "L0_attn_ln_b", "L0_ffn_gate_w", "L0_ffn_gate_b",
        "L0_ffn_w1", "L0_ffn_b1", "L0_ffn_w2", "L0_ffn_b2", "L0_ffn_gamma", "L0_ffn_beta"]


def _tables():
    import numpy as np

    two_pi = 2.0 * np.pi
    t, f = np.arange(T), np.arange(BINS)
    angle = two_pi * ((t[:, None] * f[None, :]) % T) / T
    cos, sin = np.cos(angle), np.sin(angle)
    dft = np.concatenate([cos, cos, cos, -sin, -sin, -sin], axis=1).reshape(P, TC, 6 * BINS)
    phase = np.zeros((FEATS, T + 2 * P))
    phase[0:BINS, 0:T] = sin.T
    phase[BINS:2 * BINS, 0:T] = cos.T
    phase[2 * BINS:, 0:T] = 1.0
    return {"dft": dft.astype(np.float32), "phase": phase.astype(np.float32), "ident": np.eye(P, dtype=np.float32),
            "rank": np.arange(E, 0, -1).astype(np.float32)}


def kernel(**inputs):
    import numpy as np
    import concourse.bacc as bacc
    from concourse.bass_utils import run_bass_kernel_spmd

    nc = bacc.Bacc("TRN2", target_bir_lowering=False, num_devices=1)
    named = {name: np.ascontiguousarray(inputs[name]) for name in _INS}
    named.update(_tables())
    arrays, args = {}, []
    for name, a in named.items():
        arrays[f"in_{name}"] = a
        args.append(nc.dram_tensor(f"in_{name}", a.shape, mybir.dt.from_np(a.dtype), kind="ExternalInput").ap())
    args.append(nc.dram_tensor("out_h", (ROWS, T, D), F32, kind="ExternalOutput").ap())
    build(nc, *args)
    r = run_bass_kernel_spmd(nc, [arrays], core_ids=[0])
    return r.results[0]["out_h"]
```
